# Optimizing a Trainium2 kernel written in Bass

```python
import numpy as np
import jax
import jax.numpy as jnp

def _softmax(x, axis=-1):
    return jax.nn.softmax(x, axis=axis)

def _gelu(x):
    return jax.nn.gelu(x, approximate=True)

def _silu(x):
    return jax.nn.silu(x)

def _sigmoid(x):
    return jax.nn.sigmoid(x)

def _layernorm(x, axis=-1, eps=1e-05):
    m = jnp.mean(x, axis=axis, keepdims=True)
    v = jnp.var(x, axis=axis, keepdims=True)
    return (x - m) / jnp.sqrt(v + eps)

def _scatter_add(tgt, idx, src, axis=0):
    return tgt.at[idx].add(src)

def _segment_sum(src, seg, n):
    return jax.ops.segment_sum(src, seg, n)
kernel_name = 'mk_cond_seq_d1_seqx_r4_234aa5'

def setup_inputs(seed: int=0):
    np.random.seed(seed)
    _w = jnp.asarray

    def _rec_inputs():
        import jax
        import jax.numpy as jnp
        _rk = jax.random.key(seed)
        x = -0.0003929 + 0.9999 * jax.random.normal(jax.random.fold_in(_rk, 1), (32, 64, 256), jnp.float32)
        _lenS = 64 - jax.random.randint(jax.random.fold_in(_rk, 7), (32,), 0, max(1, 64 // 4) + 1, jnp.int32)
        _lenS2 = 64 - jax.random.randint(jax.random.fold_in(_rk, 8), (32,), 0, max(1, 64 // 4) + 1, jnp.int32)
        cond_2048 = 0.00782532 + 1.00527 * jax.random.normal(jax.random.fold_in(_rk, 11), (32, 512), jnp.float32)
        _validS = jnp.arange(64)[None, :] < _lenS[:, None]
        _validS2 = jnp.arange(64)[None, :] < _lenS2[:, None]
        _causal = jnp.tril(jnp.ones((64, 64), dtype=bool))
        mask_BxS_ik0 = jnp.where(jnp.broadcast_to(_validS[:, :], (32, 64)), 0, 1).astype(jnp.int32)
        return (x, cond_2048, mask_BxS_ik0)
    x, cond_2048, mask_BxS_ik0 = _rec_inputs()

    def _L0_cond_setup():
        import jax, jax.numpy as jnp
        import numpy as np
        H = 16
        LN_EPS = 1e-05

        def _layernorm(x, scale, bias):
            mu = jnp.mean(x, axis=-1, keepdims=True)
            var = jnp.var(x, axis=-1, keepdims=True)
            return (x - mu) * jax.lax.rsqrt(var + LN_EPS) * scale + bias
        key = jax.random.key(seed)
        ks = jax.random.split(key, 8)
        B, T, D, E = (4, 1024, 256, 512)
        s = 0.02
        return {'x': jax.random.normal(ks[0], (B, T, D), jnp.float32), 'emb': jax.random.normal(ks[1], (B, E), jnp.float32), 'src_mask': jax.random.randint(ks[2], (B, T), 0, 2).astype(jnp.int32), 'norm_scale': jnp.ones((D,), jnp.float32), 'norm_bias': jnp.zeros((D,), jnp.float32), 'Wq': jax.random.normal(ks[3], (D, D), jnp.float32) * s, 'bq': jnp.zeros((D,), jnp.float32), 'Wk': jax.random.normal(ks[4], (D, D), jnp.float32) * s, 'bk': jnp.zeros((D,), jnp.float32), 'Wv': jax.random.normal(ks[5], (D, D), jnp.float32) * s, 'bv': jnp.zeros((D,), jnp.float32), 'film_emb_W': jax.random.normal(ks[6], (E, 2 * D), jnp.float32) * s, 'film_emb_b': jnp.zeros((2 * D,), jnp.float32), 'film_norm_scale': jnp.ones((D,), jnp.float32), 'film_norm_bias': jnp.zeros((D,), jnp.float32), 'film_out_W': jax.random.normal(ks[7], (D, D), jnp.float32) * s, 'film_out_b': jnp.zeros((D,), jnp.float32)}
    _L0_cond_all = _L0_cond_setup()
    _L0_cond_in = {k: v for k, v in _L0_cond_all.items() if k in ('norm_scale', 'norm_bias', 'Wq', 'bq', 'Wk', 'bk', 'Wv', 'bv', 'film_emb_W', 'film_emb_b', 'film_norm_scale', 'film_norm_bias', 'film_out_W', 'film_out_b')}
    del _L0_cond_all
    return {'x': x, 'cond_2048': cond_2048, 'mask_BxS_ik0': mask_BxS_ik0, 'L0_cond_norm_scale': _L0_cond_in['norm_scale'], 'L0_cond_norm_bias': _L0_cond_in['norm_bias'], 'L0_cond_Wq': _L0_cond_in['Wq'], 'L0_cond_bq': _L0_cond_in['bq'], 'L0_cond_Wk': _L0_cond_in['Wk'], 'L0_cond_bk': _L0_cond_in['bk'], 'L0_cond_Wv': _L0_cond_in['Wv'], 'L0_cond_bv': _L0_cond_in['bv'], 'L0_cond_film_emb_W': _L0_cond_in['film_emb_W'], 'L0_cond_film_emb_b': _L0_cond_in['film_emb_b'], 'L0_cond_film_norm_scale': _L0_cond_in['film_norm_scale'], 'L0_cond_film_norm_bias': _L0_cond_in['film_norm_bias'], 'L0_cond_film_out_W': _L0_cond_in['film_out_W'], 'L0_cond_film_out_b': _L0_cond_in['film_out_b']}

def reference(x, cond_2048, mask_BxS_ik0, L0_cond_norm_scale, L0_cond_norm_bias, L0_cond_Wq, L0_cond_bq, L0_cond_Wk, L0_cond_bk, L0_cond_Wv, L0_cond_bv, L0_cond_film_emb_W, L0_cond_film_emb_b, L0_cond_film_norm_scale, L0_cond_film_norm_bias, L0_cond_film_out_W, L0_cond_film_out_b):
    import jax
    import jax.numpy as jnp

    def _L0_cond_ref(x, emb, src_mask, norm_scale, norm_bias, Wq, bq, Wk, bk, Wv, bv, film_emb_W, film_emb_b, film_norm_scale, film_norm_bias, film_out_W, film_out_b):
        import jax, jax.numpy as jnp
        import numpy as np
        H = 16
        LN_EPS = 1e-05

        def _layernorm(x, scale, bias):
            mu = jnp.mean(x, axis=-1, keepdims=True)
            var = jnp.var(x, axis=-1, keepdims=True)
            return (x - mu) * jax.lax.rsqrt(var + LN_EPS) * scale + bias
        B, T, D = x.shape
        dh = D // H
        xn = _layernorm(x, norm_scale, norm_bias)
        q = xn @ Wq + bq
        k = xn @ Wk + bk
        v = xn @ Wv + bv
        mask = (src_mask == 1)[:, :, None]
        k = jnp.where(mask, -jnp.inf, k)
        v = jnp.where(mask, 0.0, v)
        q = q.reshape(B, T, H, dh).transpose(0, 2, 1, 3)
        k = k.reshape(B, T, H, dh).transpose(0, 2, 1, 3)
        v = v.reshape(B, T, H, dh).transpose(0, 2, 1, 3)
        q = jax.nn.softmax(q, axis=-1)
        k = jax.nn.softmax(k, axis=2)
        attn = jnp.einsum('bhse,bhsd->bhed', k, v)
        y = jnp.einsum('bhtd,bhed->bhte', q, attn)
        y = y.transpose(0, 2, 1, 3).reshape(B, T, D)
        emb_out = jax.nn.silu(emb) @ film_emb_W + film_emb_b
        scale, shift = jnp.split(emb_out, 2, axis=-1)
        h = _layernorm(y, film_norm_scale, film_norm_bias) * (1.0 + scale[:, None, :]) + shift[:, None, :]
        h = jax.nn.silu(h) @ film_out_W + film_out_b
        return x + h
    x = _L0_cond_ref(x, cond_2048, mask_BxS_ik0, L0_cond_norm_scale, L0_cond_norm_bias, L0_cond_Wq, L0_cond_bq, L0_cond_Wk, L0_cond_bk, L0_cond_Wv, L0_cond_bv, L0_cond_film_emb_W, L0_cond_film_emb_b, L0_cond_film_norm_scale, L0_cond_film_norm_bias, L0_cond_film_out_W, L0_cond_film_out_b)
    return x

_drawn_inputs = setup_inputs


def setup_inputs(seed=0):
    import zlib

    import numpy as np

    out = dict(_drawn_inputs(seed))
    spreads = {'L0_cond_norm_scale': (1.0, 0.6),
     'L0_cond_norm_bias': (0.0, 0.1),
     'L0_cond_bq': (0.0, 0.336),
     'L0_cond_bk': (0.0, 0.8),
     'L0_cond_bv': (0.0, 0.1),
     'L0_cond_film_emb_b': (0.0, 0.279),
     'L0_cond_film_norm_scale': (1.0, 0.2),
     'L0_cond_film_norm_bias': (0.0, 0.43),
     'L0_cond_film_out_b': (0.0, 0.1)}
    factors = {}
    for name, (base, spread) in spreads.items():
        noise = np.random.default_rng([zlib.crc32(name.encode()), seed]).standard_normal(out[name].shape)
        drawn = base * np.exp(spread * noise) if base else spread * noise
        out[name] = jnp.asarray(drawn.astype(out[name].dtype))
    for name, factor in factors.items():
        out[name] = (out[name] * factor).astype(out[name].dtype)
    return out
```

```python
from contextlib import ExitStack

import concourse.bass as bass
from concourse import mybir

F32 = mybir.dt.float32
F32R = mybir.dt.float32r
I32 = mybir.dt.int32
ALU = mybir.AluOpType
ACT = mybir.ActivationFunctionType
X = mybir.AxisListType.X

P = 128
EPS = 1e-5
MASKED = -1e30
MASKED_EXP = -3e38


class Unit:

    def __init__(self, pair, side):
        self.pair, self.side = pair, side

    def back(self, n):
        return Unit(self.pair + (self.side - n) // 2, (self.side - n) % 2)

    def times(self, n, plus=0):
        return self.pair * (2 * n) + (self.side * n + plus)

    def within(self, units):
        return not isinstance(self.pair, int) or 0 <= self.times(1) < units


def wait(engine, semaphore, value):
    if not isinstance(value, int) or value > 0:
        engine.wait_ge(semaphore, value)


def build(nc, x, cond, mask, norm_scale, norm_bias, wq, bq, wk, bk, wv, bv, film_w, film_b,
          film_scale, film_bias, out_w, out_b, consts, out):
    B, T, D = x.shape
    E = cond.shape[1]
    HEAD = 16
    H = D // HEAD
    KD = D // P
    KE = E // P
    TILES = 2
    UT = TILES * P
    UNITS = B * T // UT
    UB = UT // T
    TB = P // T
    PAIR = 2 * HEAD
    G = P // PAIR
    V0, K0, O0 = D, 2 * D, 3 * D
    ROWS = PAIR + 1
    STEPS = UNITS + 3
    LOOP = (4, UNITS - 2)
    assert KD == 2 and UB == 4 and P % T == 0 and H * HEAD == D

    x_u = x.rearrange("b t d -> (b t) d").rearrange("(u j p) d -> p u j d", j=TILES, p=P)
    out_u = out.rearrange("b t d -> (b t) d").rearrange("(u j p) d -> p u j d", j=TILES, p=P)

    with ExitStack() as ctx:
        def sb(name, shape, dt=F32):
            return ctx.enter_context(nc.sbuf_tensor(name, shape, dt))

        def sem(name):
            return ctx.enter_context(nc.semaphore(name))

        def bank(name):
            return ctx.enter_context(nc.psum_tensor(name, [P, 512], F32))

        const = sb("const", [P, P + PAIR + P // HEAD])
        ident = const[:, 0:P]
        head_mask = const[:, P:P + PAIR]
        head_ones = const[:, P + PAIR:P + PAIR + P // HEAD]
        w_raw = sb("w_raw", [P, KD, 4 * D])
        w_hi = sb("w_hi", [P, KD, 4 * D], F32R)
        w_lo = sb("w_lo", [P, KD, 4 * D], F32R)
        w_full = sb("w_full", [P, KD, 4 * D])
        VECS = 6 * KD
        vec_rows = sb("vec_rows", [VECS, P])
        cols = sb("cols", [P, VECS])
        n_scale, n_bias, f_scale, f_bias = (cols[:, i * KD:(i + 1) * KD] for i in range(4))
        emb_b = cols[:, 4 * KD:6 * KD]
        emb_b1 = sb("emb_b1", [P, 2 * KD])
        nb_wide = sb("nb_wide", [P, KD, ROWS])
        b_raw = sb("b_raw", [ROWS, 4 * D])
        b_full = sb("b_full", [ROWS, 4 * D])
        b_rows = sb("b_rows", [ROWS, 4 * D], F32R)
        one_rows = sb("one_rows", [ROWS, P], F32R)
        kt_rows = sb("kt_rows", [65, D], F32R)
        tok_rows = sb("tok_rows", [65, B * T], F32R)
        mask_raw = sb("mask_raw", [65, B * T], I32)
        film_raw = sb("film_raw", [P, KE, 2 * D])
        cond_s = sb("cond_s", [B, E])
        cond_t = sb("cond_t", [B, E])
        cond_silu = sb("cond_silu", [B, E])
        condT = sb("condT", [P, KE, B])
        film_1 = sb("film_1", [P, KD, B])
        film_2 = sb("film_2", [P, KD, B])
        film_g = sb("film_g", [P, KD, B])
        film_s = sb("film_s", [P, KD, B])
        power = sb("power", [P, TILES])

        def two(name, shape, dt=F32):
            return [sb(f"{name}{i}", shape, dt) for i in range(2)]

        xa = two("xa", [P, TILES, D])
        xr = two("xr", [P, TILES, D])
        bn = two("bn", [P, TILES, 6])
        mv = two("mv", [P, TILES, 2])
        var_e = two("var_e", [P, TILES])
        neg_mu = two("neg_mu", [P, TILES])
        rstd = two("rstd", [P, TILES])
        shift = two("shift", [P, TILES])
        z = two("z", [P, TILES, D])
        z_hi = two("z_hi", [P, KD, UT], F32R)
        z_lo = two("z_lo", [P, KD, UT], F32R)
        k_max = two("k_max", [P, KD * UB])
        k_sum = two("k_sum", [P, KD * UB])
        k_rec = two("k_rec", [P, KD * UB])
        k_exp = two("k_exp", [P, KD, UT])
        k_soft = two("k_soft", [P, KD, UT])
        q_max = two("q_max", [P, TILES, H])
        q_sub = two("q_sub", [P, TILES, D])
        q_exp = two("q_exp", [P, TILES, D])
        v = two("v", [P, TILES, D])
        qk_t = two("qk_t", [P, TILES, 2, KD, P])
        a_diag = two("a_diag", [P, TB, TILES, KD, P])
        q_rec = two("q_rec", [P, TILES, H])
        y = two("y", [P, TILES, D])
        bn2 = two("bn2", [P, TILES, 6])
        mv2 = two("mv2", [P, TILES, 2])
        var_e2 = two("var_e2", [P, TILES])
        neg_mu2 = two("neg_mu2", [P, TILES])
        rstd2 = two("rstd2", [P, TILES])
        shift2 = two("shift2", [P, TILES])
        yn = two("yn", [P, TILES, D])
        hp = two("hp", [P, KD, UT])
        th = two("th", [P, KD, UT])
        h2 = two("h2", [P, KD, UT])
        h_hi = two("h_hi", [P, KD, UT], F32R)
        h_lo = two("h_lo", [P, KD, UT], F32R)
        res = two("res", [P, TILES, D])

        ps_z, ps_k, ps_qv0, ps_qv1, ps_t0, ps_t1, ps_a, ps_y = [bank(f"ps{i}") for i in range(8)]
        ps_qv = [ps_qv0, ps_qv1]
        ps_t = [ps_t0, ps_t1]
        ps_h = ps_t
        ps_o = ps_y
        A_COLS = TILES * KD * PAIR
        a_bank = [ps_a, ps_y]
        den_ps = ps_a[:, 256:256 + TILES * H].rearrange("p (j h) -> p j h", j=TILES)

        s_vec, s_vecps = sem("s_vec"), sem("s_vecps")
        s_const, s_cols, s_wk, s_w, s_brow, s_wo, s_mask, s_cond, s_film = map(
            sem, ["s_const", "s_cols", "s_wk", "s_w", "s_brow", "s_wo", "s_mask", "s_cond", "s_film"])
        s_zeros, s_power, s_full, s_split, s_nbw, s_brps, s_bfull, s_brdy, s_krows, s_maskrow = map(
            sem, ["s_zeros", "s_power", "s_full", "s_split", "s_nbw", "s_brps", "s_bfull", "s_brdy",
                  "s_krows", "s_maskrow"])
        s_ctanh, s_csilu, s_ctps, s_ct, s_fps, s_f1, s_filmdone = map(
            sem, ["s_ctanh", "s_csilu", "s_ctps", "s_ct", "s_fps", "s_f1", "s_filmdone"])
        x_in = [sem("x_in0"), sem("x_in1")]
        r_in = [sem("r_in0"), sem("r_in1")]
        stored = [sem("stored0"), sem("stored1")]
        bn_done, aggr_done, stats_x, rstd_x, shift_x, z_done = map(
            sem, ["bn_done", "aggr_done", "stats_x", "rstd_x", "shift_x", "z_done"])
        zt_full, zhi_done, zlo_done = map(sem, ["zt_full", "zhi_done", "zlo_done"])
        kt_full, kmax_done, kexp_done, krec_done, ksoft_done = map(
            sem, ["kt_full", "kmax_done", "kexp_done", "krec_done", "ksoft_done"])
        qv_full, qmax_done, qsub_done, qexp_done, v_done = map(
            sem, ["qv_full", "qmax_done", "qsub_done", "qexp_done", "v_done"])
        t_full, t_read = map(sem, ["t_full", "t_read"])
        a_full, a_read = map(sem, ["a_full", "a_read"])
        y_full, qrec_done, y_read = map(sem, ["y_full", "qrec_done", "y_read"])
        bn2_done, aggr2_done, stats_y, rstd_y, shift_y, yn_done = map(
            sem, ["bn2_done", "aggr2_done", "stats_y", "rstd_y", "shift_y", "yn_done"])
        h_full, film_act, film_dve, tanh_done, silu_done, hhi_done, hlo_done = map(
            sem, ["h_full", "film_act", "film_dve", "tanh_done", "silu_done", "hhi_done", "hlo_done"])
        o_full, res_done = map(sem, ["o_full", "res_done"])

        block = ctx.enter_context(nc.Block())

        def steps(engine, step):
            for s in range(LOOP[0]):
                step(Unit(s // 2, s % 2))
            with engine.Fori(LOOP[0] // 2, LOOP[1] // 2) as pair:
                step(Unit(pair, 0))
                step(Unit(pair, 1))
            for s in range(LOOP[1], STEPS):
                step(Unit(s // 2, s % 2))

        @block.sync
        def _(sp):
            def load_x(u):
                if u.within(UNITS):
                    wait(sp, z_done, u.times(TILES, -TILES))
                    sp.dma_start(xa[u.side][:], x_u[:, u.times(1)]).then_inc(x_in[u.side], 16)

            load_x(Unit(0, 0))
            for i, (vec, n) in enumerate(((norm_scale, KD), (norm_bias, KD), (film_scale, KD), (film_bias, KD),
                                          (film_b, 2 * KD))):
                sp.dma_start(vec_rows[i * KD:i * KD + n, :], vec.rearrange("(k p) -> k p", p=P)).then_inc(s_vec, 16)
            sp.dma_start(w_raw[:, :, K0:K0 + D], wk.rearrange("(k p) n -> p k n", p=P)).then_inc(s_wk, 16)
            sp.dma_start(mask_raw[64:65, :], mask.rearrange("(a b) t -> a (b t)", a=1)).then_inc(s_mask, 16)
            sp.dma_start(w_raw[:, :, 0:D], wq.rearrange("(k p) n -> p k n", p=P)).then_inc(s_w, 16)
            sp.dma_start(w_raw[:, :, V0:V0 + D], wv.rearrange("(k p) n -> p k n", p=P)).then_inc(s_w, 16)
            load_x(Unit(0, 1))
            for i, w in enumerate((bq, bv, bk, out_b)):
                sp.dma_start(b_raw[:, i * D:(i + 1) * D],
                             w.rearrange("(a n) -> a n", a=1).to_broadcast([ROWS, D])
                             ).then_inc(s_brow, 16)
            sp.dma_start(cond_s[:], cond).then_inc(s_cond, 16)
            sp.dma_start(film_raw[:], film_w.rearrange("(k p) n -> p k n", p=P)).then_inc(s_film, 16)
            sp.dma_start(w_raw[:, :, O0:O0 + D], out_w.rearrange("(k p) n -> p k n", p=P)).then_inc(s_wo, 16)

            def step(s):
                load_x(s.back(-2))
                u = s.back(2)
                if u.within(UNITS):
                    wait(sp, res_done, u.times(1, -1))
                    sp.dma_start(xr[u.side][:], x_u[:, u.times(1)]).then_inc(r_in[u.side], 16)
                u = s.back(3)
                if u.within(UNITS):
                    wait(sp, res_done, u.times(1, 1))
                    sp.dma_start(out_u[:, u.times(1)], res[u.side][:]).then_inc(stored[u.side], 16)

            steps(sp, step)
            for side in range(2):
                sp.wait_ge(stored[side], 16 * UNITS // 2)

        @block.gpsimd
        def _(pool):
            nc.gpsimd.memset(power[:], -0.5).then_inc(s_power, 1)
            nc.gpsimd.memset(tok_rows[:].bitcast(F32), 0.0).then_inc(s_zeros, 1)
            nc.gpsimd.memset(kt_rows[:].bitcast(F32), 0.0).then_inc(s_zeros, 1)
            nc.gpsimd.memset(one_rows[:].bitcast(F32), 0.0).then_inc(s_zeros, 1)
            pool.wait_ge(s_zeros, 3)
            for row in (0, 32):
                nc.gpsimd.memset(tok_rows[row:row + 1, :].bitcast(F32), 1.0).then_inc(s_zeros, 1)
                nc.gpsimd.memset(one_rows[row:row + 1, :].bitcast(F32), 1.0).then_inc(s_zeros, 1)
            nc.gpsimd.memset(kt_rows[64:65, :].bitcast(F32), 1.0).then_inc(s_zeros, 1)

            def normalise(u, stats, var, negative, scale, scale_done, offset, offset_done, used, src, dst, done):
                wait(pool, stats, u.times(1, 1))
                nc.gpsimd.tensor_tensor(scale[u.side][:], var[u.side][:], power[:], ALU.pow).then_inc(scale_done, 1)
                wait(pool, scale_done, u.times(1, 1))
                nc.gpsimd.tensor_tensor(offset[u.side][:], negative[u.side][:], scale[u.side][:],
                                        ALU.mult).then_inc(offset_done, 1)
                wait(pool, offset_done, u.times(1, 1))
                wait(pool, used, u.times(1, -1))
                for j in range(TILES):
                    nc.gpsimd.tensor_scalar(dst[u.side][:, j], src[u.side][:, j], scale[u.side][:, j:j + 1],
                                            offset[u.side][:, j:j + 1], ALU.mult, ALU.add).then_inc(done, 1)

            def z_of(u):
                normalise(u, stats_x, var_e, neg_mu, rstd, rstd_x, shift, shift_x, zt_full, xa, z, z_done)

            pool.wait_ge(s_power, 1)
            pool.wait_ge(s_zeros, 8)
            z_of(Unit(0, 0))
            z_of(Unit(0, 1))

            def step(s):
                u = s
                if u.within(UNITS):
                    wait(pool, krec_done, u.times(1, 1))
                    wait(pool, t_full, u.times(TILES, -TILES))
                    nc.gpsimd.tensor_tensor(
                        k_soft[u.side][:].rearrange("p k (b t) -> p (k b) t", t=T),
                        k_exp[u.side][:].rearrange("p k (b t) -> p (k b) t", t=T),
                        k_rec[u.side][:, :, None].to_broadcast([P, KD * UB, T]), ALU.mult).then_inc(ksoft_done, 1)
                u = s.back(2)
                if u.within(UNITS):
                    wait(pool, hhi_done, u.times(1, 1))
                    wait(pool, o_full, u.times(1, -1))
                    nc.gpsimd.tensor_tensor(h_lo[u.side][:], h2[u.side][:], h_hi[u.side][:].bitcast(F32),
                                            ALU.subtract).then_inc(hlo_done, 1)
                u = s.back(-2)
                if u.within(UNITS):
                    z_of(u)
                u = s.back(1)
                if u.within(UNITS):
                    normalise(u, stats_y, var_e2, neg_mu2, rstd2, rstd_y, shift2, shift_y, h_full, y, yn, yn_done)

            steps(pool, step)

        @block.scalar
        def _(act):
            act.dma_start(const[:], consts).then_inc(s_const, 16)

            def z_high(u):
                wait(act, zt_full, u.times(1, 1))
                wait(act, qv_full, u.times(TILES, -TILES))
                nc.scalar.activation(z_hi[u.side][:], ps_z[:].rearrange("p (k t) -> p k t", k=KD),
                                     ACT.Copy).then_inc(zhi_done, 1)

            z_high(Unit(0, 0))
            act.wait_ge(s_cond, 16)
            nc.scalar.activation(cond_t[:], cond_s[:], ACT.Tanh, scale=0.5).then_inc(s_ctanh, 1)

            def step(s):
                u = s.back(1)
                if u.within(UNITS):
                    wait(act, y_full, u.times(1, -1))
                    for j in range(TILES):
                        wait(act, t_full, u.times(TILES, j + 1))
                        nc.scalar.activation(qk_t[u.side][:, j].rearrange("p a k t -> p (a k t)"), ps_t[j][:],
                                             ACT.Copy).then_inc(t_read, 1)
                u = s
                if u.within(UNITS):
                    wait(act, kmax_done, u.times(1, 1))
                    wait(act, ksoft_done, u.times(1, -1))
                    for k in range(KD):
                        for b in range(UB):
                            n = k * UB + b
                            last = nc.scalar.activation(
                                k_exp[u.side][:, k, b * T:(b + 1) * T], ps_k[:, n * T:(n + 1) * T], ACT.Exp,
                                bias=k_max[u.side][:, n:n + 1], accum_out=k_sum[u.side][:, n:n + 1])
                    last.then_inc(kexp_done, 1)

                def v_of(u, j):
                    wait(act, qsub_done, u.times(TILES, j + 1))
                    wait(act, a_full, u.times(1, -1))
                    nc.scalar.activation(v[u.side][:, j], ps_qv[j][:, V0:V0 + D], ACT.Copy).then_inc(v_done, 1)

                if u.within(UNITS):
                    v_of(u, 0)
                u = s.back(2)
                if u.within(UNITS):
                    wait(act, h_full, u.times(1, 1))
                    wait(act, silu_done, u.times(1, -1))
                    for b in range(UB):
                        at = u.times(UB, b)
                        last = nc.scalar.activation(
                            hp[u.side][:, 0, b * T:(b + 1) * T], ps_h[0][:, b * T:(b + 1) * T], ACT.Identity,
                            bias=film_s[:, 0, bass.ds(at, 1)], scale=film_g[:, 0, bass.ds(at, 1)])
                    last.then_inc(film_act, 1)
                    wait(act, film_act, u.times(1, 1))
                    wait(act, film_dve, u.times(1, 1))
                    nc.scalar.activation(th[u.side][:], hp[u.side][:], ACT.Tanh, scale=0.5).then_inc(tanh_done, 1)
                    wait(act, silu_done, u.times(1, 1))
                    wait(act, o_full, u.times(1, -1))
                    nc.scalar.activation(h_hi[u.side][:], h2[u.side][:], ACT.Copy).then_inc(hhi_done, 1)
                u = s
                if u.within(UNITS):
                    v_of(u, 1)
                    wait(act, qsub_done, u.times(TILES, TILES))
                    wait(act, t_full, u.times(TILES, -TILES))
                    nc.scalar.activation(q_exp[u.side][:], q_sub[u.side][:], ACT.Exp).then_inc(qexp_done, 1)
                u = s.back(-1)
                if u.within(UNITS):
                    z_high(u)

            steps(act, step)

        @block.vector
        def _(dve):
            def stats(u, src, ready, ready_at, used, bn_t, bn_sem, mv_t, aggr_sem, var, negative, done):
                wait(dve, ready, ready_at)
                wait(dve, used, u.times(1, -1))
                for j in range(TILES):
                    last = nc.vector.bn_stats(bn_t[u.side][:, j], src[u.side][:, j])
                last.then_inc(bn_sem, 1)
                wait(dve, bn_sem, u.times(1, 1))
                for j in range(TILES):
                    last = nc.vector.bn_aggr(mv_t[u.side][:, j], bn_t[u.side][:, j])
                last.then_inc(aggr_sem, 1)
                wait(dve, aggr_sem, u.times(1, 1))
                nc.vector.tensor_scalar(var[u.side][:], mv_t[u.side][:, :, 1], EPS, None, ALU.add)
                nc.vector.tensor_scalar(negative[u.side][:], mv_t[u.side][:, :, 0], -1.0, None,
                                        ALU.mult).then_inc(done, 1)

            def x_stats(u):
                stats(u, xa, x_in[u.side], (u.pair + 1) * 16, shift_x, bn, bn_done, mv, aggr_done, var_e,
                      neg_mu, stats_x)

            def z_low(u):
                wait(dve, zhi_done, u.times(1, 1))
                nc.vector.tensor_tensor(z_lo[u.side][:], ps_z[:].rearrange("p (k t) -> p k t", k=KD),
                                        z_hi[u.side][:].bitcast(F32), ALU.subtract).then_inc(zlo_done, 1)

            def split(c, at):
                dve.wait_ge(s_full, at)
                nc.vector.tensor_copy(w_hi[:, :, c:c + D], w_full[:, :, c:c + D]).then_inc(s_full, 1)
                dve.wait_ge(s_full, at + 1)
                nc.vector.tensor_tensor(w_lo[:, :, c:c + D], w_full[:, :, c:c + D],
                                        w_hi[:, :, c:c + D].bitcast(F32), ALU.subtract).then_inc(s_split, 1)

            def scaled(c):
                for k in range(KD):
                    last = nc.vector.tensor_scalar(w_full[:, k, c:c + D], w_raw[:, k, c:c + D],
                                                   n_scale[:, k:k + 1], None, ALU.mult)
                last.then_inc(s_full, 1)

            x_stats(Unit(0, 0))
            dve.wait_ge(s_vecps, 1)
            nc.vector.tensor_copy(cols[:], ps_t0[:, 0:VECS]).then_inc(s_cols, 1)
            dve.wait_ge(s_cols, 1)
            dve.wait_ge(s_wk, 16)
            scaled(K0)
            split(K0, 1)
            x_stats(Unit(0, 1))
            for k in range(KD):
                last = nc.vector.tensor_copy(nb_wide[:, k], n_bias[:, k:k + 1].to_broadcast([P, ROWS]))
            last.then_inc(s_nbw, 1)
            dve.wait_ge(s_mask, 16)
            dve.wait_ge(s_zeros, 8)
            nc.vector.tensor_scalar(tok_rows[64:65, :], mask_raw[64:65, :], 1.0, MASKED, ALU.is_equal,
                                    ALU.mult).then_inc(s_maskrow, 1)
            dve.wait_ge(s_brow, 64)
            dve.wait_ge(s_brps, 1)
            nc.vector.tensor_tensor(b_full[:, 0:2 * D], b_raw[:, 0:2 * D], ps_a[0:ROWS, :], ALU.add)
            nc.vector.tensor_tensor(b_full[:, K0:K0 + D], b_raw[:, K0:K0 + D], ps_y[0:ROWS, 0:D], ALU.add)
            nc.vector.tensor_copy(b_full[:, O0:O0 + D], b_raw[:, O0:O0 + D]).then_inc(s_bfull, 1)
            dve.wait_ge(s_bfull, 1)
            nc.vector.tensor_copy(b_rows[:], b_full[:]).then_inc(s_bfull, 1)
            dve.wait_ge(s_bfull, 2)
            nc.vector.tensor_tensor(b_rows[32:33, :], b_full[32:33, :], b_rows[32:33, :].bitcast(F32),
                                    ALU.subtract).then_inc(s_brdy, 1)
            dve.wait_ge(s_brdy, 1)
            nc.vector.tensor_copy(kt_rows[0:1, :], b_rows[0:1, K0:K0 + D].bitcast(F32))
            nc.vector.tensor_copy(kt_rows[32:33, :], b_rows[32:33, K0:K0 + D].bitcast(F32)).then_inc(s_krows, 1)
            dve.wait_ge(s_w, 32)
            scaled(0)
            split(0, 3)
            scaled(V0)
            split(V0, 5)
            z_low(Unit(0, 0))
            dve.wait_ge(s_ctanh, 1)
            nc.vector.scalar_tensor_tensor(cond_silu[:], cond_t[:], 1.0, cond_s[:], ALU.add,
                                           ALU.mult).then_inc(s_csilu, 1)
            dve.wait_ge(s_wo, 16)
            nc.vector.tensor_scalar(w_full[:, :, O0:O0 + D], w_raw[:, :, O0:O0 + D], 0.5, None,
                                    ALU.mult).then_inc(s_full, 1)
            split(O0, 7)
            nc.vector.tensor_scalar(emb_b1[:], emb_b, 1.0, None, ALU.add).then_inc(s_f1, 1)
            dve.wait_ge(s_ctps, 1)
            nc.vector.tensor_copy(condT[:], ps_t1[:, 0:KE * B].rearrange("p (k b) -> p k b", k=KE)).then_inc(s_ct, 1)
            for side in range(2):
                last = nc.vector.memset(a_diag[side][:], 0.0)
            last.then_inc(s_f1, 1)
            dve.wait_ge(s_f1, 2)
            dve.wait_ge(s_fps, 1)
            for k in range(KD):
                nc.vector.tensor_scalar(film_1[:, k], ps_t0[:, k * B:(k + 1) * B], 0.5, emb_b1[:, k:k + 1],
                                        ALU.mult, ALU.add)
                last = nc.vector.tensor_scalar(film_2[:, k], ps_t0[:, (KD + k) * B:(KD + k + 1) * B], 0.5,
                                               emb_b[:, KD + k:KD + k + 1], ALU.mult, ALU.add)
            last.then_inc(s_f1, 1)
            dve.wait_ge(s_f1, 3)
            for k in range(KD):
                nc.vector.tensor_scalar(film_g[:, k], film_1[:, k], f_scale[:, k:k + 1], None, ALU.mult)
                last = nc.vector.scalar_tensor_tensor(film_s[:, k], film_1[:, k], f_bias[:, k:k + 1],
                                                      film_2[:, k], ALU.mult, ALU.add)
            last.then_inc(s_filmdone, 1)

            def q_of(u, j):
                wait(dve, qv_full, u.times(TILES, j + 1))
                wait(dve, qexp_done, u.times(1, -1))
                q = ps_qv[j][:, 0:D].rearrange("p (h c) -> p h c", c=HEAD)
                nc.vector.tensor_reduce(q_max[u.side][:, j], q, X, ALU.max).then_inc(qmax_done, 1)
                wait(dve, qmax_done, u.times(TILES, j + 1))
                nc.vector.tensor_tensor(q_sub[u.side][:, j].rearrange("p (h c) -> p h c", c=HEAD), q,
                                        q_max[u.side][:, j, :, None].to_broadcast([P, H, HEAD]),
                                        ALU.subtract).then_inc(qsub_done, 1)

            def step(s):
                u = s
                if u.within(UNITS):
                    wait(dve, kt_full, u.times(1, 1))
                    wait(dve, kexp_done, u.times(1, -1))
                    nc.vector.tensor_reduce(k_max[u.side][:], ps_k[:].rearrange("p (n t) -> p n t", t=T), X,
                                            ALU.max, negate=True).then_inc(kmax_done, 1)
                u = s.back(3)
                if u.within(UNITS):
                    wait(dve, o_full, u.times(1, 1))
                    wait(dve, r_in[u.side], (u.pair + 1) * 16)
                    wait(dve, stored[u.side], u.pair * 16)
                    nc.vector.tensor_tensor(res[u.side][:].rearrange("p j d -> p (j d)"), ps_o[:],
                                            xr[u.side][:].rearrange("p j d -> p (j d)"), ALU.add).then_inc(res_done, 1)
                u = s
                if u.within(UNITS):
                    q_of(u, 0)
                u = s.back(1)
                if u.within(UNITS):
                    wait(dve, a_full, u.times(1, 1))
                    wait(dve, y_full, u.times(1, -1))
                    for i in range(TB):
                        for g in range(G):
                            r = slice(g * PAIR, (g + 1) * PAIR)
                            last = nc.vector.tensor_tensor(
                                a_diag[u.side][r, i, :, :, r].rearrange("p j k c -> p (j k) c"),
                                a_bank[i][r, 0:A_COLS].rearrange("p (n c) -> p n c", c=PAIR),
                                head_mask[r, None, :].to_broadcast([PAIR, TILES * KD, PAIR]), ALU.mult)
                    last.then_inc(a_read, 1)
                u = s
                if u.within(UNITS):
                    wait(dve, kexp_done, u.times(1, 1))
                    wait(dve, ksoft_done, u.times(1, -1))
                    nc.vector.reciprocal(k_rec[u.side][:], k_sum[u.side][:]).then_inc(krec_done, 1)
                u = s.back(2)
                if u.within(UNITS):
                    wait(dve, h_full, u.times(1, 1))
                    for b in range(UB):
                        at = u.times(UB, b)
                        last = nc.vector.tensor_scalar(
                            hp[u.side][:, 1, b * T:(b + 1) * T], ps_h[1][:, b * T:(b + 1) * T],
                            film_g[:, 1, bass.ds(at, 1)], film_s[:, 1, bass.ds(at, 1)], ALU.mult, ALU.add)
                    last.then_inc(film_dve, 1)
                    wait(dve, tanh_done, u.times(1, 1))
                    wait(dve, hlo_done, u.times(1, -1))
                    nc.vector.scalar_tensor_tensor(h2[u.side][:].rearrange("p k t -> p (k t)"),
                                                   th[u.side][:].rearrange("p k t -> p (k t)"), 1.0,
                                                   hp[u.side][:].rearrange("p k t -> p (k t)"),
                                                   ALU.add, ALU.mult).then_inc(silu_done, 1)
                u = s
                if u.within(UNITS):
                    q_of(u, 1)
                u = s.back(-1)
                if u.within(UNITS):
                    z_low(u)
                u = s.back(-2)
                if u.within(UNITS):
                    x_stats(u)
                u = s.back(1)
                if u.within(UNITS):
                    wait(dve, y_full, u.times(1, 1))
                    nc.vector.reciprocal(q_rec[u.side][:], den_ps).then_inc(qrec_done, 1)
                    wait(dve, qrec_done, u.times(1, 1))
                    wait(dve, yn_done, u.times(TILES, -TILES))
                    nc.vector.tensor_tensor(
                        y[u.side][:].rearrange("p j (h c) -> p (j h) c", c=HEAD),
                        ps_y[:].rearrange("p (n c) -> p n c", c=HEAD),
                        q_rec[u.side][:].rearrange("p j h -> p (j h)")[:, :, None].to_broadcast([P, TILES * H, HEAD]),
                        ALU.mult).then_inc(y_read, 1)
                    stats(u, y, y_read, u.times(1, 1), shift_y, bn2, bn2_done, mv2, aggr2_done, var_e2,
                          neg_mu2, stats_y)

            steps(dve, step)

        @block.tensor
        def _(pe):
            def z_transposed(u):
                wait(pe, z_done, u.times(TILES, TILES))
                wait(pe, zlo_done, u.times(1, 0))
                for k in range(KD):
                    for j in range(TILES):
                        last = nc.tensor.transpose(ps_z[:, k * UT + j * P:k * UT + (j + 1) * P],
                                                   z[u.side][:, j, k * P:(k + 1) * P], ident)
                last.then_inc(zt_full, 1)

            def parts(hi, lo, other_hi, other_lo):
                return ((hi, other_hi), (hi, other_lo), (lo, other_hi))

            pe.wait_ge(s_const, 16)
            pe.wait_ge(s_vec, 16 * 5)
            nc.tensor.transpose(ps_t0[:, 0:VECS], vec_rows[:], ident[0:VECS, 0:VECS]).then_inc(s_vecps, 1)
            z_transposed(Unit(0, 0))
            pe.wait_ge(s_nbw, 1)
            pe.wait_ge(s_w, 32)
            for k in range(KD):
                nc.tensor.matmul(ps_a[0:ROWS, :], nb_wide[:, k], w_raw[:, k, 0:2 * D], start=k == 0, stop=k == KD - 1)
            for k in range(KD):
                last = nc.tensor.matmul(ps_y[0:ROWS, 0:D], nb_wide[:, k], w_raw[:, k, K0:K0 + D],
                                        start=k == 0, stop=k == KD - 1)
            last.then_inc(s_brps, 1)
            pe.wait_ge(s_csilu, 1)
            for k in range(KE):
                last = nc.tensor.transpose(ps_t1[:, k * B:(k + 1) * B], cond_silu[:, k * P:(k + 1) * P],
                                           ident[0:B, 0:B])
            last.then_inc(s_ctps, 1)
            pe.wait_ge(s_ct, 1)
            pe.wait_ge(s_film, 16)
            for c in range(2 * KD):
                for k in range(KE):
                    last = nc.tensor.matmul(ps_t0[:, c * B:(c + 1) * B], film_raw[:, k, c * P:(c + 1) * P],
                                            condT[:, k], start=k == 0, stop=k == KE - 1)
            last.then_inc(s_fps, 1)
            pe.wait_ge(s_split, 4)
            pe.wait_ge(s_krows, 1)
            pe.wait_ge(s_maskrow, 1)
            pe.wait_ge(s_zeros, 8)
            pe.wait_ge(s_filmdone, 1)

            def qv(u, j):
                wait(pe, qsub_done, u.times(TILES, j + 1 - TILES))
                wait(pe, v_done, u.times(TILES, j + 1 - TILES))
                t = slice(j * P, (j + 1) * P)
                nc.tensor.matmul(ps_qv[j][:], one_rows[:], b_rows[:, 0:2 * D], start=True, stop=False)
                for k in range(KD):
                    for n, (a, w) in enumerate(parts(z_hi, z_lo, w_hi, w_lo)):
                        last = nc.tensor.matmul(ps_qv[j][:], a[u.side][:, k, t], w[:, k, 0:2 * D],
                                                start=False, stop=k == KD - 1 and n == 2)
                last.then_inc(qv_full, 1)

            def step(s):
                u = s
                if u.within(UNITS):
                    wait(pe, zhi_done, u.times(1, 1))
                    wait(pe, zlo_done, u.times(1, 1))
                    wait(pe, kexp_done, u.times(1, 0))
                    for c in range(KD):
                        dst = ps_k[:, c * UT:(c + 1) * UT]
                        ch = slice(K0 + c * P, K0 + (c + 1) * P)
                        for k in range(KD):
                            for n, (a, w) in enumerate(parts(z_hi, z_lo, w_hi, w_lo)):
                                nc.tensor.matmul(dst, w[:, k, ch], a[u.side][:, k], start=k == 0 and n == 0,
                                                 stop=False)
                        last = nc.tensor.matmul(dst, kt_rows[:, c * P:(c + 1) * P],
                                                tok_rows[:, bass.ds(u.times(UT), UT)], start=False, stop=True)
                    last.then_inc(kt_full, 1)
                u = s.back(3)
                if u.within(UNITS):
                    wait(pe, hlo_done, u.times(1, 1))
                    y_unit = u.back(-1) if u.back(-1).within(UNITS) else u
                    wait(pe, y_read, y_unit.times(1, 1))
                    for j in range(TILES):
                        dst = ps_o[:, j * D:(j + 1) * D]
                        t = slice(j * P, (j + 1) * P)
                        for k in range(KD):
                            for n, (a, w) in enumerate(parts(h_hi, h_lo, w_hi, w_lo)):
                                nc.tensor.matmul(dst, a[u.side][:, k, t], w[:, k, O0:O0 + D],
                                                 start=k == 0 and n == 0, stop=False)
                        last = nc.tensor.matmul(dst, one_rows[:], b_rows[:, O0:O0 + D], start=False, stop=True)
                    last.then_inc(o_full, 1)
                u = s.back(1)
                if u.within(UNITS):
                    wait(pe, qexp_done, u.times(1, 1))
                    wait(pe, ksoft_done, u.times(1, 1))
                    wait(pe, film_act, u.times(1, -1))
                    wait(pe, film_dve, u.times(1, -1))
                    for j in range(TILES):
                        wait(pe, t_read, u.times(TILES, j + 1 - TILES))
                        for k in range(KD):
                            nc.tensor.transpose(ps_t[j][:, k * P:(k + 1) * P],
                                                q_exp[u.side][:, j, k * P:(k + 1) * P], ident)
                        for k in range(KD):
                            last = nc.tensor.transpose(ps_t[j][:, D + k * P:D + (k + 1) * P],
                                                       k_soft[u.side][:, k, j * P:(j + 1) * P], ident)
                        last.then_inc(t_full, 1)
                if s.within(UNITS):
                    qv(s, 0)
                if u.within(UNITS):
                    wait(pe, t_read, u.times(TILES, TILES))
                    wait(pe, v_done, u.times(TILES, TILES))
                    wait(pe, a_read, u.times(1, 0))
                    wait(pe, qrec_done, u.times(1, 0))
                    wait(pe, y_read, u.times(1, 0))
                    wait(pe, res_done, u.times(1, -1))
                    for j in range(TILES):
                        for k in range(KD):
                            for i in range(TB):
                                for g in range(G):
                                    r = slice(i * T, (i + 1) * T)
                                    c = slice(k * P + g * PAIR, k * P + (g + 1) * PAIR)
                                    at = (j * KD + k) * PAIR
                                    last = nc.tensor.matmul(
                                        a_bank[i][g * PAIR:(g + 1) * PAIR, at:at + PAIR], v[u.side][r, j, c],
                                        qk_t[u.side][r, j, 1].rearrange("p k t -> p (k t)")[:, c],
                                        start=True, stop=True)
                    last.then_inc(a_full, 1)
                h = s.back(2)
                if h.within(UNITS):
                    wait(pe, yn_done, h.times(TILES, TILES))
                    if not u.within(UNITS):
                        wait(pe, t_read, UNITS * TILES)
                    for k in range(KD):
                        for j in range(TILES):
                            last = nc.tensor.transpose(ps_h[k][:, j * P:(j + 1) * P],
                                                       yn[h.side][:, j, k * P:(k + 1) * P], ident)
                    last.then_inc(h_full, 1)
                if s.within(UNITS):
                    qv(s, 1)
                n = s.back(-1)
                if n.within(UNITS):
                    z_transposed(n)
                if u.within(UNITS):
                    wait(pe, a_read, u.times(1, 1))
                    for j in range(TILES):
                        for k in range(KD):
                            nc.tensor.matmul(den_ps[:, j, k * H // KD:(k + 1) * H // KD], qk_t[u.side][:, j, 0, k],
                                             head_ones, start=True, stop=True)
                        for k in range(KD):
                            for i in range(TB):
                                r = slice(i * T, (i + 1) * T)
                                last = nc.tensor.matmul(ps_y[r, j * D + k * P:j * D + (k + 1) * P],
                                                        qk_t[u.side][:, j, 0, k, r], a_diag[u.side][:, i, j, k],
                                                        start=True, stop=True)
                    last.then_inc(y_full, 1)

            steps(pe, step)


_INS = ["x", "cond_2048", "mask_BxS_ik0", "L0_cond_norm_scale", "L0_cond_norm_bias", "L0_cond_Wq", "L0_cond_bq",
        "L0_cond_Wk", "L0_cond_bk", "L0_cond_Wv", "L0_cond_bv", "L0_cond_film_emb_W", "L0_cond_film_emb_b",
        "L0_cond_film_norm_scale", "L0_cond_film_norm_bias", "L0_cond_film_out_W", "L0_cond_film_out_b"]


def kernel(**inputs):
    import numpy as np
    import concourse.bacc as bacc
    from concourse.bass_utils import run_bass_kernel_spmd

    nc = bacc.Bacc("TRN2", target_bir_lowering=False, num_devices=1)
    arrays, args = {}, []
    for name in _INS:
        a = np.ascontiguousarray(inputs[name])
        arrays[name] = a
        args.append(nc.dram_tensor(name, a.shape, mybir.dt.from_np(a.dtype), kind="ExternalInput").ap())
    p, head = np.arange(128), 16
    consts = np.concatenate([np.eye(128), p[:, None] % 32 // head == np.arange(32)[None] // head,
                             p[:, None] // head == np.arange(128 // head)[None]], axis=1).astype(np.float32)
    arrays["consts"] = consts
    args.append(nc.dram_tensor("consts", consts.shape, F32, kind="ExternalInput").ap())
    shape = inputs["x"].shape
    args.append(nc.dram_tensor("out", shape, F32, kind="ExternalOutput").ap())
    build(nc, *args)
    return run_bass_kernel_spmd(nc, [arrays], core_ids=[0]).results[0]["out"]
```

```python
from contextlib import ExitStack

import concourse.bass as bass
from concourse import mybir

F32 = mybir.dt.float32
F32R = mybir.dt.float32r
I32 = mybir.dt.int32
ALU = mybir.AluOpType
ACT = mybir.ActivationFunctionType
X = mybir.AxisListType.X

P = 128
EPS = 1e-5
MASKED = -1e30
MASKED_EXP = -3e38


class Unit:

    def __init__(self, pair, side):
        self.pair, self.side = pair, side

    def back(self, n):
        return Unit(self.pair + (self.side - n) // 2, (self.side - n) % 2)

    def times(self, n, plus=0):
        return self.pair * (2 * n) + (self.side * n + plus)

    def first(self):
        return isinstance(self.pair, int) and self.times(1) == 0

    def within(self, units):
        return not isinstance(self.pair, int) or 0 <= self.times(1) < units


def wait(engine, semaphore, value):
    if not isinstance(value, int) or value > 0:
        engine.wait_ge(semaphore, value)


def build(nc, x, cond, mask, norm_scale, norm_bias, wq, bq, wk, bk, wv, bv, film_w, film_b,
          film_scale, film_bias, out_w, out_b, consts, out):
    B, T, D = x.shape
    E = cond.shape[1]
    HEAD = 16
    H = D // HEAD
    KD = D // P
    KE = E // P
    TILES = 2
    UT = TILES * P
    UNITS = B * T // UT
    UB = UT // T
    TB = P // T
    PAIR = 2 * HEAD
    G = P // PAIR
    V0, K0, O0 = D, 2 * D, 3 * D
    ROWS = PAIR + 1
    STEPS = UNITS + 3
    LOOP = (4, UNITS - 2)
    assert KD == 2 and UB == 4 and P % T == 0 and H * HEAD == D

    x_u = x.rearrange("b t d -> (b t) d").rearrange("(u j p) d -> p u j d", j=TILES, p=P)
    out_u = out.rearrange("b t d -> (b t) d").rearrange("(u j p) d -> p u j d", j=TILES, p=P)

    with ExitStack() as ctx:
        def sb(name, shape, dt=F32):
            return ctx.enter_context(nc.sbuf_tensor(name, shape, dt))

        def sem(name):
            return ctx.enter_context(nc.semaphore(name))

        def bank(name):
            return ctx.enter_context(nc.psum_tensor(name, [P, 512], F32))

        const = sb("const", [P, P + PAIR + P // HEAD])
        ident = const[:, 0:P]
        head_mask = const[:, P:P + PAIR]
        head_ones = const[:, P + PAIR:P + PAIR + P // HEAD]
        w_raw = sb("w_raw", [P, KD, 4 * D])
        w_hi = sb("w_hi", [P, KD, 4 * D], F32R)
        w_lo = sb("w_lo", [P, KD, 4 * D], F32R)
        VECS = 6 * KD
        vec_rows = sb("vec_rows", [VECS, P])
        cols = sb("cols", [P, VECS])
        n_scale, n_bias, f_scale, f_bias = (cols[:, i * KD:(i + 1) * KD] for i in range(4))
        emb_b = cols[:, 4 * KD:6 * KD]
        emb_b1 = sb("emb_b1", [P, 2 * KD])
        nb_wide = sb("nb_wide", [P, KD, ROWS])
        b_raw = sb("b_raw", [ROWS, 4 * D])
        b_full = sb("b_full", [ROWS, 4 * D])
        wv_full = sb("wv_full", [P, KD, D])
        b_rows = sb("b_rows", [ROWS, 4 * D], F32R)
        one_rows = sb("one_rows", [ROWS, P], F32R)
        kt_rows = sb("kt_rows", [65, D], F32R)
        tok_rows = sb("tok_rows", [65, B * T], F32R)
        MASK_P = B * T // P
        mask_raw = sb("mask_raw", [MASK_P, P], I32)
        mask_row = sb("mask_row", [MASK_P, P], F32R)
        film_raw = sb("film_raw", [P, KE, 2 * D])
        cond_s = sb("cond_s", [B, E])
        cond_t = sb("cond_t", [B, E])
        cond_silu = sb("cond_silu", [B, E])
        condT = sb("condT", [P, KE, B])
        emb_rows = sb("emb_rows", [P, P])
        film_1 = sb("film_1", [P, KD, B])
        film_2 = sb("film_2", [P, KD, B])
        film_g = sb("film_g", [P, KD, B])
        film_s = sb("film_s", [P, KD, B])
        power = sb("power", [P, TILES])

        def two(name, shape, dt=F32):
            return [sb(f"{name}{i}", shape, dt) for i in range(2)]

        xa = two("xa", [P, TILES, D])
        xr = two("xr", [P, TILES, D])
        bn = two("bn", [P, TILES, 6])
        mv = two("mv", [P, TILES, 2])
        var_e = two("var_e", [P, TILES])
        neg_rstd = two("neg_rstd", [P, TILES])
        rstd = two("rstd", [P, TILES])
        shift = two("shift", [P, TILES])
        z = two("z", [P, TILES, D])
        z_hi = two("z_hi", [P, KD, UT], F32R)
        z_lo = two("z_lo", [P, KD, UT], F32R)
        k_max = two("k_max", [P, KD * UB])
        k_sum = two("k_sum", [P, KD * UB])
        k_rec = two("k_rec", [P, KD * UB])
        k_exp = two("k_exp", [P, KD, UT])
        k_soft = two("k_soft", [P, KD, UT])
        q_max = two("q_max", [P, TILES, H])
        q_sub = two("q_sub", [P, TILES, D])
        q_exp = two("q_exp", [P, TILES, D])
        v = two("v", [P, TILES, D])
        qk_t = two("qk_t", [P, TILES, 2, KD, P])
        a_pair = two("a_pair", [P, TB, TILES, KD, PAIR])
        a_diag = two("a_diag", [P, TB, TILES, KD, P + G * 2])
        q_rec = two("q_rec", [P, TILES, H])
        y = two("y", [P, TILES, D])
        bn2 = two("bn2", [P, TILES, 6])
        mv2 = two("mv2", [P, TILES, 2])
        var_e2 = two("var_e2", [P, TILES])
        neg_rstd2 = two("neg_rstd2", [P, TILES])
        rstd2 = two("rstd2", [P, TILES])
        shift2 = two("shift2", [P, TILES])
        yn = two("yn", [P, TILES, D])
        h_scaled = two("h_scaled", [P, KD, UT])
        hp = two("hp", [P, KD, UT])
        th = two("th", [P, KD, UT])
        h2 = two("h2", [P, KD, UT])
        h_hi = two("h_hi", [P, KD, UT], F32R)
        h_lo = two("h_lo", [P, KD, UT], F32R)
        res = two("res", [P, TILES, D])

        ps_z, ps_k = bank("ps_z"), bank("ps_k")
        ps_qv, ps_t, ps_yo = (ctx.enter_context(nc.psum_tensor(name, [P, 2, 512], F32))
                              for name in ("ps_qv", "ps_t", "ps_yo"))
        A_COLS = TILES * KD * PAIR
        YC = P + G * 2

        s_vec, s_vecps = sem("s_vec"), sem("s_vecps")
        s_const, s_cols, s_wk, s_w, s_brow, s_wo, s_mask, s_cond, s_film = map(
            sem, ["s_const", "s_cols", "s_wk", "s_w", "s_brow", "s_wo", "s_mask", "s_cond", "s_film"])
        s_ones, s_diag0, s_tok, s_bqv, s_heads = map(sem, ["s_ones", "s_diag0", "s_tok", "s_bqv", "s_heads"])
        s_zeros, s_power, s_whi, s_split, s_nbw, s_brps, s_bfull, s_brdy, s_krows, s_maskrow = map(
            sem, ["s_zeros", "s_power", "s_whi", "s_split", "s_nbw", "s_brps", "s_bfull", "s_brdy",
                  "s_krows", "s_maskrow"])
        s_split_v = sem("s_split_v")
        s_maskf, s_bhi, s_emb, s_embt = map(sem, ["s_maskf", "s_bhi", "s_emb", "s_embt"])
        s_ctanh, s_csilu, s_ctps, s_ct, s_fps, s_f1, s_filmdone = map(
            sem, ["s_ctanh", "s_csilu", "s_ctps", "s_ct", "s_fps", "s_f1", "s_filmdone"])
        x_in = [sem("x_in0"), sem("x_in1")]
        r_in = [sem("r_in0"), sem("r_in1")]
        stored = [sem("stored0"), sem("stored1")]
        bn_done, stats_x, var_x, rstd_x, neg_x, shift_x, z_done = map(
            sem, ["bn_done", "stats_x", "var_x", "rstd_x", "neg_x", "shift_x", "z_done"])
        zt_full, zhi_done, zlo_done = map(sem, ["zt_full", "zhi_done", "zlo_done"])
        kt_full, kmax_done, kexp_done, krec_done, ksoft_done = map(
            sem, ["kt_full", "kmax_done", "kexp_done", "krec_done", "ksoft_done"])
        qv_full, qmax_done, qsub_done, qexp_done, v_done = map(
            sem, ["qv_full", "qmax_done", "qsub_done", "qexp_done", "v_done"])
        t_full, t_read = map(sem, ["t_full", "t_read"])
        a_full, a_read, diag_act, diag_dve = map(sem, ["a_full", "a_read", "diag_act", "diag_dve"])
        y_full, qrec_done, y_read = map(sem, ["y_full", "qrec_done", "y_read"])
        bn2_done, stats_y, var_y, rstd_y, neg_y, shift_y, yn_done = map(
            sem, ["bn2_done", "stats_y", "var_y", "rstd_y", "neg_y", "shift_y", "yn_done"])
        h_full, film_mul, film_add, tanh_done, silu_done, hhi_done, hlo_done = map(
            sem, ["h_full", "film_mul", "film_add", "tanh_done", "silu_done", "hhi_done", "hlo_done"])
        o_full, res_done = map(sem, ["o_full", "res_done"])

        block = ctx.enter_context(nc.Block())

        def steps(engine, step, late_setup=lambda: None):
            step(Unit(0, 0))
            late_setup()
            for s in range(1, LOOP[0]):
                step(Unit(s // 2, s % 2))
            with engine.Fori(LOOP[0] // 2, LOOP[1] // 2) as pair:
                step(Unit(pair, 0))
                step(Unit(pair, 1))
            for s in range(LOOP[1], STEPS):
                step(Unit(s // 2, s % 2))

        def diagonal(u, g):
            r = slice(g * PAIR, (g + 1) * PAIR)
            return (a_diag[u.side][r, :, :, :, r].rearrange("p i j k c -> p (i j k) c"),
                    a_pair[u.side][r].rearrange("p i j k c -> p (i j k) c"))

        @block.sync
        def _(sp):
            def load_x(u):
                if u.within(UNITS):
                    wait(sp, z_done, u.times(1, -1))
                    sp.dma_start(xa[u.side][:], x_u[:, u.times(1)]).then_inc(x_in[u.side], 16)

            load_x(Unit(0, 0))
            for i, (vec, n) in enumerate(((norm_scale, KD), (norm_bias, KD), (film_scale, KD), (film_bias, KD),
                                          (film_b, 2 * KD))):
                sp.dma_start(vec_rows[i * KD:i * KD + n, :], vec.rearrange("(k p) -> k p", p=P)).then_inc(s_vec, 16)
            sp.dma_start(mask_raw[:], mask.rearrange("(a b) t -> a (b t)", a=MASK_P)).then_inc(s_mask, 16)
            for c, w in ((0, wq), (V0, wv)):
                sp.dma_start(w_raw[:, :, c:c + D], w.rearrange("(k p) n -> p k n", p=P)).then_inc(s_w, 16)
            load_x(Unit(0, 1))
            for dst, w in ((b_raw[:, K0:K0 + D], bk), (b_raw[:, 0:D], bq), (b_raw[:, V0:V0 + D], bv),
                           (b_full[:, O0:O0 + D], out_b)):
                sp.dma_start(dst, w.rearrange("(a n) -> a n", a=1).to_broadcast([ROWS, D])).then_inc(s_brow, 16)
            sp.dma_start(cond_s[:], cond).then_inc(s_cond, 16)
            sp.dma_start(film_raw[:], film_w.rearrange("(k p) n -> p k n", p=P)).then_inc(s_film, 16)
            sp.dma_start(w_raw[:, :, O0:O0 + D], out_w.rearrange("(k p) n -> p k n", p=P)).then_inc(s_wo, 16)

            def step(s):
                load_x(s.back(-2))
                u = s.back(2)
                if u.within(UNITS):
                    wait(sp, res_done, u.times(1, -1))
                    sp.dma_start(xr[u.side][:], x_u[:, u.times(1)]).then_inc(r_in[u.side], 16)
                u = s.back(3)
                if u.within(UNITS):
                    wait(sp, res_done, u.times(1, 1))
                    sp.dma_start(out_u[:, u.times(1)], res[u.side][:]).then_inc(stored[u.side], 16)

            steps(sp, step)
            for side in range(2):
                sp.wait_ge(stored[side], 16 * UNITS // 2)

        @block.gpsimd
        def _(pool):
            nc.gpsimd.memset(power[:], -0.5).then_inc(s_power, 1)
            nc.gpsimd.memset(kt_rows[:].bitcast(F32), 0.0).then_inc(s_zeros, 1)
            nc.gpsimd.memset(one_rows[:].bitcast(F32), 0.0).then_inc(s_zeros, 1)
            pool.wait_ge(s_zeros, 2)
            for row in (0, 32):
                nc.gpsimd.memset(one_rows[row:row + 1, :].bitcast(F32), 1.0).then_inc(s_ones, 1)
            nc.gpsimd.memset(kt_rows[64:65, :].bitcast(F32), 1.0).then_inc(s_ones, 1)

            def scale_and_shift(u, stats, mv_t, var, var_done, scale, scale_done, negative, negative_done,
                                offset, offset_done, used):
                wait(pool, stats, u.times(1, 1))
                wait(pool, used, u.times(1, -1))
                nc.gpsimd.tensor_scalar(var[u.side][:], mv_t[u.side][:, :, 1], EPS, None, ALU.add).then_inc(var_done, 1)
                wait(pool, var_done, u.times(1, 1))
                nc.gpsimd.tensor_tensor(scale[u.side][:], var[u.side][:], power[:], ALU.pow).then_inc(scale_done, 1)
                wait(pool, scale_done, u.times(1, 1))
                nc.gpsimd.tensor_scalar(negative[u.side][:], scale[u.side][:], -1.0, None,
                                        ALU.mult).then_inc(negative_done, 1)
                wait(pool, negative_done, u.times(1, 1))
                nc.gpsimd.tensor_tensor(offset[u.side][:], mv_t[u.side][:, :, 0], negative[u.side][:],
                                        ALU.mult).then_inc(offset_done, 1)

            def z_of(u):
                scale_and_shift(u, stats_x, mv, var_e, var_x, rstd, rstd_x, neg_rstd, neg_x, shift, shift_x, z_done)
                wait(pool, shift_x, u.times(1, 1))
                wait(pool, zt_full, u.times(1, -1))
                for j in range(TILES):
                    last = nc.gpsimd.tensor_scalar(z[u.side][:, j], xa[u.side][:, j], rstd[u.side][:, j:j + 1],
                                                   shift[u.side][:, j:j + 1], ALU.mult, ALU.add)
                last.then_inc(z_done, 1)

            pool.wait_ge(s_power, 1)
            pool.wait_ge(s_ones, 3)
            z_of(Unit(0, 0))
            pool.wait_ge(s_whi, 2)
            nc.gpsimd.tensor_tensor(w_lo[:, :, V0:V0 + D], wv_full[:], w_hi[:, :, V0:V0 + D].bitcast(F32),
                                    ALU.subtract).then_inc(s_split_v, 1)
            z_of(Unit(0, 1))
            for side in range(2):
                last = nc.gpsimd.memset(a_diag[side][:], 0.0)
            last.then_inc(s_diag0, 1)

            def step(s):
                h = s.back(2)
                if h.within(UNITS):
                    scale_and_shift(h, stats_y, mv2, var_e2, var_y, rstd2, rstd_y, neg_rstd2, neg_y, shift2, shift_y,
                                    yn_done)
                if s.back(-2).within(UNITS):
                    z_of(s.back(-2))
                if h.within(UNITS):
                    wait(pool, film_mul, h.times(1, 1))
                    wait(pool, silu_done, h.times(1, -1))
                    nc.gpsimd.tensor_tensor(
                        hp[h.side][:].rearrange("p k (b t) -> p k b t", t=T),
                        h_scaled[h.side][:].rearrange("p k (b t) -> p k b t", t=T),
                        film_s[:, :, bass.ds(h.times(UB), UB), None].to_broadcast([P, KD, UB, T]),
                        ALU.add).then_inc(film_add, 1)
                if s.within(UNITS):
                    wait(pool, krec_done, s.times(1, 1))
                    wait(pool, t_full, s.times(TILES, -TILES))
                    nc.gpsimd.tensor_tensor(
                        k_soft[s.side][:].rearrange("p k (b t) -> p (k b) t", t=T),
                        k_exp[s.side][:].rearrange("p k (b t) -> p (k b) t", t=T),
                        k_rec[s.side][:, :, None].to_broadcast([P, KD * UB, T]), ALU.mult).then_inc(ksoft_done, 1)
                if h.within(UNITS):
                    wait(pool, hhi_done, h.times(1, 1))
                    wait(pool, o_full, h.times(1, -1))
                    nc.gpsimd.tensor_tensor(h_lo[h.side][:], h2[h.side][:], h_hi[h.side][:].bitcast(F32),
                                            ALU.subtract).then_inc(hlo_done, 1)
            steps(pool, step)

        @block.scalar
        def _(act):
            act.dma_start(const[:], consts).then_inc(s_const, 16)
            act.dma_start(w_raw[:, :, K0:K0 + D], wk.rearrange("(k p) n -> p k n", p=P)).then_inc(s_wk, 16)

            def weights_high(c):
                for k in range(KD):
                    last = nc.scalar.activation(w_hi[:, k, c:c + D], w_raw[:, k, c:c + D], ACT.Copy,
                                                scale=n_scale[:, k:k + 1])
                last.then_inc(s_whi, 1)

            def z_high(u):
                wait(act, zt_full, u.times(1, 1))
                wait(act, qv_full, u.times(TILES, -TILES))
                nc.scalar.activation(z_hi[u.side][:], ps_z[:].rearrange("p (k t) -> p k t", k=KD),
                                     ACT.Copy).then_inc(zhi_done, 1)

            act.wait_ge(s_cols, 1)
            act.wait_ge(s_wk, 16)
            weights_high(K0)
            act.wait_ge(s_maskf, 1)
            act.wait_ge(s_tok, 1)
            act.dma_start(tok_rows[64:65, :].bitcast(F32), mask_row[:].bitcast(F32)).then_inc(s_maskrow, 16)
            z_high(Unit(0, 0))
            act.wait_ge(s_w, 32)
            for k in range(KD):
                nc.scalar.activation(wv_full[:, k], w_raw[:, k, V0:V0 + D], ACT.Copy, scale=n_scale[:, k:k + 1])
            weights_high(V0)
            weights_high(0)
            act.wait_ge(s_cond, 16)
            nc.scalar.activation(cond_t[:], cond_s[:], ACT.Tanh, scale=0.5).then_inc(s_ctanh, 1)

            act.wait_ge(s_bqv, 1)
            for c, n in ((0, 2 * D), (O0, D)):
                last = nc.scalar.activation(b_rows[:, c:c + n], b_full[:, c:c + n], ACT.Copy)
            last.then_inc(s_bhi, 1)
            act.wait_ge(s_ctps, 1)
            nc.scalar.activation(condT[:], ps_yo[:, 1, 0:KE * B].rearrange("p (k b) -> p k b", k=KE),
                                 ACT.Copy).then_inc(s_ct, 1)

            def late_setup():
                act.wait_ge(s_wo, 16)
                nc.scalar.activation(w_hi[:, :, O0:O0 + D], w_raw[:, :, O0:O0 + D], ACT.Copy,
                                     scale=0.5).then_inc(s_whi, 1)

            def v_of(u, j):
                wait(act, qsub_done, u.times(TILES, j + 1))
                wait(act, a_full, u.times(1, -1))
                nc.scalar.activation(v[u.side][:, j], ps_qv[:, j, V0:V0 + D], ACT.Copy).then_inc(v_done, 1)

            def step(s):
                a, h = s.back(1), s.back(2)
                if a.within(UNITS):
                    wait(act, y_full, a.times(1, -1))
                    for j in range(TILES):
                        wait(act, t_full, a.times(TILES, j + 1))
                        nc.scalar.activation(qk_t[a.side][:, j].rearrange("p a k t -> p (a k t)"), ps_t[:, j],
                                             ACT.Copy).then_inc(t_read, 1)
                if s.back(-1).within(UNITS):
                    z_high(s.back(-1))
                if h.within(UNITS):
                    wait(act, shift_y, h.times(1, 1))
                    wait(act, h_full, h.times(1, -1))
                    for j in range(TILES):
                        last = nc.scalar.activation(yn[h.side][:, j], y[h.side][:, j], ACT.Identity,
                                                    bias=shift2[h.side][:, j:j + 1], scale=rstd2[h.side][:, j:j + 1])
                    last.then_inc(yn_done, 1)
                if s.within(UNITS):
                    wait(act, kmax_done, s.times(1, 1))
                    wait(act, ksoft_done, s.times(1, -1))
                    for k in range(KD):
                        for b in range(UB):
                            n = k * UB + b
                            last = nc.scalar.activation(
                                k_exp[s.side][:, k, b * T:(b + 1) * T], ps_k[:, n * T:(n + 1) * T], ACT.Exp,
                                bias=k_max[s.side][:, n:n + 1], accum_out=k_sum[s.side][:, n:n + 1])
                    last.then_inc(kexp_done, 1)
                if s.within(UNITS):
                    v_of(s, 0)
                if a.within(UNITS):
                    wait(act, a_read, a.times(1, 1))
                    wait(act, y_full, a.times(1, -1))
                    for g in range(2, G):
                        last = nc.scalar.activation(*diagonal(a, g), ACT.Copy)
                    last.then_inc(diag_act, 1)
                if h.within(UNITS):
                    wait(act, film_add, h.times(1, 1))
                    nc.scalar.activation(th[h.side][:], hp[h.side][:], ACT.Tanh, scale=0.5).then_inc(tanh_done, 1)
                if s.within(UNITS):
                    v_of(s, 1)
                    wait(act, qsub_done, s.times(TILES, TILES))
                    wait(act, t_full, s.times(TILES, -TILES))
                    nc.scalar.activation(q_exp[s.side][:], q_sub[s.side][:], ACT.Exp).then_inc(qexp_done, 1)
                if h.within(UNITS):
                    wait(act, silu_done, h.times(1, 1))
                    wait(act, o_full, h.times(1, -1))
                    nc.scalar.activation(h_hi[h.side][:], h2[h.side][:], ACT.Copy).then_inc(hhi_done, 1)

            steps(act, step, late_setup)

        @block.vector
        def _(dve):
            def stats(u, src, ready, ready_at, used, bn_t, bn_sem):
                wait(dve, ready, ready_at)
                for j in range(TILES):
                    last = nc.vector.bn_stats(bn_t[u.side][:, j], src[u.side][:, j])
                last.then_inc(bn_sem, 1)

            def mean_variance(u, bn_t, bn_sem, mv_t, used, done):
                wait(dve, bn_sem, u.times(1, 1))
                wait(dve, used, u.times(1, -1))
                for j in range(TILES):
                    last = nc.vector.bn_aggr(mv_t[u.side][:, j], bn_t[u.side][:, j])
                last.then_inc(done, 1)

            def x_stats(u):
                stats(u, xa, x_in[u.side], (u.pair + 1) * 16, shift_x, bn, bn_done)

            def x_mean(u):
                mean_variance(u, bn, bn_done, mv, shift_x, stats_x)

            def z_low(u):
                wait(dve, zhi_done, u.times(1, 1))
                nc.vector.tensor_tensor(z_lo[u.side][:], ps_z[:].rearrange("p (k t) -> p k t", k=KD),
                                        z_hi[u.side][:].bitcast(F32), ALU.subtract).then_inc(zlo_done, 1)

            def weights_low(c, at):
                dve.wait_ge(s_whi, at)
                for k in range(KD):
                    last = nc.vector.scalar_tensor_tensor(w_lo[:, k, c:c + D], w_raw[:, k, c:c + D],
                                                          n_scale[:, k:k + 1], w_hi[:, k, c:c + D].bitcast(F32),
                                                          ALU.mult, ALU.subtract)
                last.then_inc(s_split, 1)

            nc.vector.memset(tok_rows[:].bitcast(F32), 1.0).then_inc(s_tok, 1)
            x_stats(Unit(0, 0))
            x_mean(Unit(0, 0))
            dve.wait_ge(s_vecps, 1)
            nc.vector.tensor_copy(cols[:], ps_t[:, 0, 0:VECS]).then_inc(s_cols, 1)
            dve.wait_ge(s_cols, 1)
            for k in range(KD):
                last = nc.vector.tensor_copy(nb_wide[:, k], n_bias[:, k:k + 1].to_broadcast([P, ROWS]))
            last.then_inc(s_nbw, 1)
            dve.wait_ge(s_mask, 16)
            nc.vector.tensor_scalar(mask_row[:], mask_raw[:], 1.0, MASKED, ALU.is_equal, ALU.mult).then_inc(s_maskf, 1)
            weights_low(K0, 1)
            x_stats(Unit(0, 1))
            x_mean(Unit(0, 1))
            z_low(Unit(0, 0))
            dve.wait_ge(s_brow, 64)
            dve.wait_ge(s_brps, 1)
            dve.wait_ge(s_ones, 3)
            kb = slice(K0, K0 + D)
            nc.vector.tensor_tensor(b_full[:, kb], b_raw[:, kb], ps_yo[0:ROWS, 1, 0:D], ALU.add).then_inc(s_bfull, 1)
            dve.wait_ge(s_bfull, 1)
            nc.vector.tensor_copy(b_rows[:, kb], b_full[:, kb])
            nc.vector.tensor_copy(kt_rows[0:1, :], b_full[0:1, kb]).then_inc(s_bfull, 1)
            dve.wait_ge(s_bfull, 2)
            nc.vector.tensor_tensor(kt_rows[32:33, :], b_full[32:33, kb], b_rows[32:33, kb].bitcast(F32),
                                    ALU.subtract).then_inc(s_krows, 1)

            weights_low(0, 3)
            dve.wait_ge(s_brps, 2)
            nc.vector.tensor_tensor(b_full[:, 0:2 * D], b_raw[:, 0:2 * D], ps_yo[0:ROWS, 0, :],
                                    ALU.add).then_inc(s_bqv, 1)
            dve.wait_ge(s_ctanh, 1)
            nc.vector.scalar_tensor_tensor(cond_silu[:], cond_t[:], 1.0, cond_s[:], ALU.add,
                                           ALU.mult).then_inc(s_csilu, 1)

            def biases_low():
                dve.wait_ge(s_bhi, 1)
                for c, n in ((0, 2 * D), (O0, D)):
                    last = nc.vector.tensor_tensor(b_rows[32:33, c:c + n], b_full[32:33, c:c + n],
                                                   b_rows[32:33, c:c + n].bitcast(F32), ALU.subtract)
                last.then_inc(s_brdy, 1)

            def late_setup():
                dve.wait_ge(s_fps, 1)
                nc.vector.tensor_copy(emb_rows[:], ps_yo[:, 0, 0:P]).then_inc(s_emb, 1)
                dve.wait_ge(s_diag0, 1)
                for side in range(2):
                    last = nc.vector.tensor_copy(
                        a_diag[side][:, :, :, :, P:YC].rearrange("p i j k h -> p (i j k) h"),
                        head_ones[:, None, :].to_broadcast([P, TB * TILES * KD, P // HEAD]))
                last.then_inc(s_heads, 1)
                dve.wait_ge(s_whi, 4)
                nc.vector.scalar_tensor_tensor(w_lo[:, :, O0:O0 + D], w_raw[:, :, O0:O0 + D], 0.5,
                                               w_hi[:, :, O0:O0 + D].bitcast(F32), ALU.mult,
                                               ALU.subtract).then_inc(s_split, 1)

            def film_setup():
                nc.vector.tensor_scalar(emb_b1[:], emb_b, 1.0, None, ALU.add).then_inc(s_f1, 1)
                dve.wait_ge(s_f1, 1)
                dve.wait_ge(s_embt, 1)
                for k in range(KD):
                    nc.vector.tensor_scalar(film_1[:, k], ps_yo[:, 1, k * B:(k + 1) * B], 0.5, emb_b1[:, k:k + 1],
                                            ALU.mult, ALU.add)
                    last = nc.vector.tensor_scalar(film_2[:, k], ps_yo[:, 1, (KD + k) * B:(KD + k + 1) * B], 0.5,
                                                   emb_b[:, KD + k:KD + k + 1], ALU.mult, ALU.add)
                last.then_inc(s_f1, 1)
                dve.wait_ge(s_f1, 2)
                for k in range(KD):
                    nc.vector.tensor_scalar(film_g[:, k], film_1[:, k], f_scale[:, k:k + 1], None, ALU.mult)
                    last = nc.vector.scalar_tensor_tensor(film_s[:, k], film_1[:, k], f_bias[:, k:k + 1],
                                                          film_2[:, k], ALU.mult, ALU.add)
                last.then_inc(s_filmdone, 1)

            def q_of(j):
                return ps_qv[:, j, 0:D].rearrange("p (h c) -> p h c", c=HEAD)

            def maximum(u, j):
                wait(dve, qv_full, u.times(TILES, j + 1))
                nc.vector.tensor_reduce(q_max[u.side][:, j], q_of(j), X, ALU.max).then_inc(qmax_done, 1)

            def less_maximum(u, j):
                wait(dve, qmax_done, u.times(TILES, j + 1))
                wait(dve, qexp_done, u.times(1, -1))
                nc.vector.tensor_tensor(q_sub[u.side][:, j].rearrange("p (h c) -> p h c", c=HEAD), q_of(j),
                                        q_max[u.side][:, j, :, None].to_broadcast([P, H, HEAD]),
                                        ALU.subtract).then_inc(qsub_done, 1)

            def step(s):
                ahead, a, h, o = s.back(-2), s.back(1), s.back(2), s.back(3)
                if s.within(UNITS):
                    wait(dve, kt_full, s.times(1, 1))
                    wait(dve, kexp_done, s.times(1, -1))
                    nc.vector.tensor_reduce(k_max[s.side][:], ps_k[:].rearrange("p (n t) -> p n t", t=T), X,
                                            ALU.max, negate=True).then_inc(kmax_done, 1)
                    if s.first():
                        biases_low()
                if a.first():
                    film_setup()
                if ahead.within(UNITS):
                    x_stats(ahead)
                    x_mean(ahead)
                if s.back(-1).within(UNITS):
                    z_low(s.back(-1))
                if o.within(UNITS):
                    wait(dve, o_full, o.times(1, 1))
                    wait(dve, r_in[o.side], (o.pair + 1) * 16)
                    wait(dve, stored[o.side], o.pair * 16)
                    nc.vector.tensor_tensor(res[o.side][:], ps_yo[:, :, 0:D], xr[o.side][:], ALU.add).then_inc(res_done, 1)
                if s.within(UNITS):
                    maximum(s, 0)
                    less_maximum(s, 0)
                if h.within(UNITS):
                    wait(dve, h_full, h.times(1, 1))
                    wait(dve, film_add, h.times(1, -1))
                    nc.vector.tensor_tensor(
                        h_scaled[h.side][:].rearrange("p k (b t) -> p k b t", t=T),
                        ps_t[:, :, 0:UT].rearrange("p k (b t) -> p k b t", t=T),
                        film_g[:, :, bass.ds(h.times(UB), UB), None].to_broadcast([P, KD, UB, T]),
                        ALU.mult).then_inc(film_mul, 1)
                if s.within(UNITS):
                    wait(dve, kexp_done, s.times(1, 1))
                    wait(dve, ksoft_done, s.times(1, -1))
                    nc.vector.reciprocal(k_rec[s.side][:], k_sum[s.side][:]).then_inc(krec_done, 1)
                if a.within(UNITS):
                    wait(dve, a_full, a.times(1, 1))
                    wait(dve, diag_act, a.times(1, -1))
                    wait(dve, diag_dve, a.times(1, -1))
                    nc.vector.tensor_tensor(
                        a_pair[a.side][:].rearrange("p i j k c -> p i (j k) c"),
                        ps_yo[:, :, 0:A_COLS].rearrange("p i (n c) -> p i n c", c=PAIR),
                        head_mask[:, None, None, :].to_broadcast([P, TB, TILES * KD, PAIR]), ALU.mult).then_inc(a_read, 1)
                if a.within(UNITS):
                    wait(dve, a_read, a.times(1, 1))
                    wait(dve, y_full, a.times(1, -1))
                    for g in range(2):
                        last = nc.vector.tensor_copy(*diagonal(a, g))
                    last.then_inc(diag_dve, 1)
                if s.within(UNITS):
                    maximum(s, 1)
                    less_maximum(s, 1)
                if h.within(UNITS):
                    wait(dve, tanh_done, h.times(1, 1))
                    wait(dve, hlo_done, h.times(1, -1))
                    nc.vector.scalar_tensor_tensor(h2[h.side][:].rearrange("p k t -> p (k t)"),
                                                   th[h.side][:].rearrange("p k t -> p (k t)"), 1.0,
                                                   hp[h.side][:].rearrange("p k t -> p (k t)"),
                                                   ALU.add, ALU.mult).then_inc(silu_done, 1)
                if a.within(UNITS):
                    wait(dve, y_full, a.times(1, 1))
                    ys = ps_yo[:, :, 0:KD * YC].rearrange("p j (k c) -> p j k c", c=YC)
                    nc.vector.reciprocal(q_rec[a.side][:].rearrange("p j (k h) -> p j k h", k=KD),
                                         ys[:, :, :, P:YC]).then_inc(qrec_done, 1)
                    wait(dve, qrec_done, a.times(1, 1))
                    wait(dve, yn_done, a.times(1, -1))
                    for j in range(TILES):
                        last = nc.vector.tensor_tensor(
                            y[a.side][:, j].rearrange("p (k h c) -> p k h c", k=KD, c=HEAD),
                            ys[:, j, :, 0:P].rearrange("p k (h c) -> p k h c", c=HEAD),
                            q_rec[a.side][:, j].rearrange("p (k h) -> p k h", k=KD)[:, :, :, None]
                            .to_broadcast([P, KD, H // KD, HEAD]), ALU.mult)
                    last.then_inc(y_read, 1)
                    stats(a, y, y_read, a.times(1, 1), shift_y, bn2, bn2_done)
                    mean_variance(a, bn2, bn2_done, mv2, shift_y, stats_y)

            steps(dve, step, late_setup)

        @block.tensor
        def _(pe):
            def z_transposed(u):
                wait(pe, z_done, u.times(1, 1))
                wait(pe, zlo_done, u.times(1, 0))
                for k in range(KD):
                    for j in range(TILES):
                        last = nc.tensor.transpose(ps_z[:, k * UT + j * P:k * UT + (j + 1) * P],
                                                   z[u.side][:, j, k * P:(k + 1) * P], ident)
                last.then_inc(zt_full, 1)

            def parts(hi, lo, other_hi, other_lo):
                return ((hi, other_hi), (hi, other_lo), (lo, other_hi))

            pe.wait_ge(s_const, 16)
            pe.wait_ge(s_vec, 16 * 5)
            nc.tensor.transpose(ps_t[:, 0, 0:VECS], vec_rows[:], ident[0:VECS, 0:VECS]).then_inc(s_vecps, 1)
            z_transposed(Unit(0, 0))
            pe.wait_ge(s_nbw, 1)
            pe.wait_ge(s_wk, 16)
            for k in range(KD):
                last = nc.tensor.matmul(ps_yo[0:ROWS, 1, 0:D], nb_wide[:, k], w_raw[:, k, K0:K0 + D],
                                        start=k == 0, stop=k == KD - 1)
            last.then_inc(s_brps, 1)
            pe.wait_ge(s_w, 32)
            for k in range(KD):
                last = nc.tensor.matmul(ps_yo[0:ROWS, 0, :], nb_wide[:, k], w_raw[:, k, 0:2 * D], start=k == 0, stop=k == KD - 1)
            last.then_inc(s_brps, 1)

            def cond_transposed():
                pe.wait_ge(s_bqv, 1)
                pe.wait_ge(s_csilu, 1)
                for k in range(KE):
                    last = nc.tensor.transpose(ps_yo[:, 1, k * B:(k + 1) * B], cond_silu[:, k * P:(k + 1) * P],
                                               ident[0:B, 0:B])
                last.then_inc(s_ctps, 1)

            def late_setup():
                pe.wait_ge(s_ct, 1)
                pe.wait_ge(s_film, 16)
                for k in range(KE):
                    for c in range(2 * KD):
                        last = nc.tensor.matmul(ps_yo[c * B:(c + 1) * B, 0, 0:P], condT[:, k],
                                                film_raw[:, k, c * P:(c + 1) * P], start=k == 0, stop=k == KE - 1)
                last.then_inc(s_fps, 1)

            def qv(u, j):
                wait(pe, qsub_done, u.times(TILES, j + 1 - TILES))
                wait(pe, v_done, u.times(TILES, j + 1 - TILES))
                if u.first():
                    pe.wait_ge(s_split, 2)
                    pe.wait_ge(s_split_v, 1)
                t = slice(j * P, (j + 1) * P)
                for k in range(KD):
                    for n, (a, w) in enumerate(parts(z_hi, z_lo, w_hi, w_lo)):
                        nc.tensor.matmul(ps_qv[:, j], a[u.side][:, k, t], w[:, k, 0:2 * D],
                                         start=k == 0 and n == 0, stop=False)
                if u.first():
                    pe.wait_ge(s_brdy, 1)
                last = nc.tensor.matmul(ps_qv[:, j], one_rows[:], b_rows[:, 0:2 * D], start=False, stop=True)
                last.then_inc(qv_full, 1)

            def step(s):
                u = s
                if u.within(UNITS):
                    wait(pe, zhi_done, u.times(1, 1))
                    wait(pe, zlo_done, u.times(1, 1))
                    wait(pe, kexp_done, u.times(1, 0))
                    if u.first():
                        pe.wait_ge(s_split, 1)
                    for c in range(KD):
                        dst = ps_k[:, c * UT:(c + 1) * UT]
                        ch = slice(K0 + c * P, K0 + (c + 1) * P)
                        for k in range(KD):
                            for n, (a, w) in enumerate(parts(z_hi, z_lo, w_hi, w_lo)):
                                nc.tensor.matmul(dst, w[:, k, ch], a[u.side][:, k], start=k == 0 and n == 0,
                                                 stop=False)
                        if u.first():
                            pe.wait_ge(s_krows, 1)
                            pe.wait_ge(s_maskrow, 16)
                            pe.wait_ge(s_ones, 3)
                        last = nc.tensor.matmul(dst, kt_rows[:, c * P:(c + 1) * P],
                                                tok_rows[:, bass.ds(u.times(UT), UT)], start=False, stop=True)
                    last.then_inc(kt_full, 1)
                    if u.first():
                        cond_transposed()
                u = s.back(1)
                if u.within(UNITS):
                    wait(pe, qexp_done, u.times(1, 1))
                    wait(pe, ksoft_done, u.times(1, 1))
                    wait(pe, film_mul, u.times(1, -1))
                    for j in range(TILES):
                        wait(pe, t_read, u.times(TILES, j + 1 - TILES))
                        for k in range(KD):
                            nc.tensor.transpose(ps_t[:, j, k * P:(k + 1) * P],
                                                q_exp[u.side][:, j, k * P:(k + 1) * P], ident)
                        for k in range(KD):
                            last = nc.tensor.transpose(ps_t[:, j, D + k * P:D + (k + 1) * P],
                                                       k_soft[u.side][:, k, j * P:(j + 1) * P], ident)
                        last.then_inc(t_full, 1)
                    if u.first():
                        pe.wait_ge(s_emb, 1)
                        nc.tensor.transpose(ps_yo[:, 1, 0:P], emb_rows[:], ident).then_inc(s_embt, 1)
                n = s.back(-1)
                if n.within(UNITS):
                    z_transposed(n)
                o = s.back(3)
                if o.within(UNITS):
                    wait(pe, hlo_done, o.times(1, 1))
                    y_unit = o.back(-1) if o.back(-1).within(UNITS) else o
                    wait(pe, y_read, y_unit.times(1, 1))
                    if o.first():
                        pe.wait_ge(s_split, 3)
                    for j in range(TILES):
                        dst = ps_yo[:, j, 0:D]
                        t = slice(j * P, (j + 1) * P)
                        for k in range(KD):
                            for n, (a, w) in enumerate(parts(h_hi, h_lo, w_hi, w_lo)):
                                nc.tensor.matmul(dst, a[o.side][:, k, t], w[:, k, O0:O0 + D],
                                                 start=k == 0 and n == 0, stop=False)
                        last = nc.tensor.matmul(dst, one_rows[:], b_rows[:, O0:O0 + D], start=False, stop=True)
                    last.then_inc(o_full, 1)
                if s.within(UNITS):
                    qv(s, 0)
                h = s.back(2)
                if h.within(UNITS):
                    wait(pe, yn_done, h.times(1, 1))
                    for k in range(KD):
                        wait(pe, t_read, (u if u.within(UNITS) else h).times(TILES, k + 1))
                        for j in range(TILES):
                            last = nc.tensor.transpose(ps_t[:, k, j * P:(j + 1) * P],
                                                       yn[h.side][:, j, k * P:(k + 1) * P], ident)
                    last.then_inc(h_full, 1)
                if u.within(UNITS):
                    wait(pe, t_read, u.times(TILES, TILES))
                    wait(pe, v_done, u.times(TILES, TILES))
                    if u.first():
                        pe.wait_ge(s_filmdone, 1)
                        pe.wait_ge(s_heads, 1)
                    wait(pe, y_read, u.times(1, 0))
                    wait(pe, res_done, u.times(1, -1))
                    for j in range(TILES):
                        for k in range(KD):
                            for i in range(TB):
                                for g in range(G):
                                    r = slice(i * T, (i + 1) * T)
                                    c = slice(k * P + g * PAIR, k * P + (g + 1) * PAIR)
                                    at = (j * KD + k) * PAIR
                                    last = nc.tensor.matmul(
                                        ps_yo[g * PAIR:(g + 1) * PAIR, i, at:at + PAIR], v[u.side][r, j, c],
                                        qk_t[u.side][r, j, 1].rearrange("p k t -> p (k t)")[:, c],
                                        start=True, stop=True)
                    last.then_inc(a_full, 1)
                if s.within(UNITS):
                    qv(s, 1)
                if u.within(UNITS):
                    wait(pe, diag_act, u.times(1, 1))
                    wait(pe, diag_dve, u.times(1, 1))
                    for j in range(TILES):
                        for k in range(KD):
                            for i in range(TB):
                                r = slice(i * T, (i + 1) * T)
                                last = nc.tensor.matmul(ps_yo[r, j, k * YC:(k + 1) * YC],
                                                        qk_t[u.side][:, j, 0, k, r], a_diag[u.side][:, i, j, k],
                                                        start=True, stop=True)
                    last.then_inc(y_full, 1)

            steps(pe, step, late_setup)


_INS = ["x", "cond_2048", "mask_BxS_ik0", "L0_cond_norm_scale", "L0_cond_norm_bias", "L0_cond_Wq", "L0_cond_bq",
        "L0_cond_Wk", "L0_cond_bk", "L0_cond_Wv", "L0_cond_bv", "L0_cond_film_emb_W", "L0_cond_film_emb_b",
        "L0_cond_film_norm_scale", "L0_cond_film_norm_bias", "L0_cond_film_out_W", "L0_cond_film_out_b"]


def kernel(**inputs):
    import numpy as np
    import concourse.bacc as bacc
    from concourse.bass_utils import run_bass_kernel_spmd

    nc = bacc.Bacc("TRN2", target_bir_lowering=False, num_devices=1)
    arrays, args = {}, []
    for name in _INS:
        a = np.ascontiguousarray(inputs[name])
        arrays[name] = a
        args.append(nc.dram_tensor(name, a.shape, mybir.dt.from_np(a.dtype), kind="ExternalInput").ap())
    p, head = np.arange(128), 16
    consts = np.concatenate([np.eye(128), p[:, None] % 32 // head == np.arange(32)[None] // head,
                             p[:, None] // head == np.arange(128 // head)[None]], axis=1).astype(np.float32)
    arrays["consts"] = consts
    args.append(nc.dram_tensor("consts", consts.shape, F32, kind="ExternalInput").ap())
    shape = inputs["x"].shape
    args.append(nc.dram_tensor("out", shape, F32, kind="ExternalOutput").ap())
    build(nc, *args)
    return run_bass_kernel_spmd(nc, [arrays], core_ids=[0]).results[0]["out"]
```

```python
from contextlib import ExitStack

import concourse.bass as bass
from concourse import mybir

F32 = mybir.dt.float32
F32R = mybir.dt.float32r
I32 = mybir.dt.int32
ALU = mybir.AluOpType
ACT = mybir.ActivationFunctionType
X = mybir.AxisListType.X

P = 128
EPS = 1e-5
MASKED = -1e30


class Unit:

    def __init__(self, pair, side):
        self.pair, self.side = pair, side

    def back(self, n):
        return Unit(self.pair + (self.side - n) // 2, (self.side - n) % 2)

    def times(self, n, plus=0):
        return self.pair * (2 * n) + (self.side * n + plus)

    def first(self):
        return isinstance(self.pair, int) and self.times(1) == 0

    def within(self, units):
        return not isinstance(self.pair, int) or 0 <= self.times(1) < units


def wait(engine, semaphore, value):
    if not isinstance(value, int) or value > 0:
        engine.wait_ge(semaphore, value)


def build(nc, x, cond, mask, norm_scale, norm_bias, wq, bq, wk, bk, wv, bv, film_w, film_b,
          film_scale, film_bias, out_w, out_b, consts, out):
    B, T, D = x.shape
    E = cond.shape[1]
    HEAD = 16
    H = D // HEAD
    KD = D // P
    KE = E // P
    TILES = 2
    UT = TILES * P
    UNITS = B * T // UT
    UB = UT // T
    TB = P // T
    PAIR = 2 * HEAD
    G = P // PAIR
    V0, K0, O0 = D, 2 * D, 3 * D
    ROWS = PAIR + 1
    STEPS = UNITS + 3
    LOOP = (4, UNITS - 2)
    assert KD == 2 and UB == 4 and P % T == 0 and H * HEAD == D

    x_u = x.rearrange("b t d -> (b t) d").rearrange("(u j p) d -> p u j d", j=TILES, p=P)
    out_u = out.rearrange("b t d -> (b t) d").rearrange("(u j p) d -> p u j d", j=TILES, p=P)

    with ExitStack() as ctx:
        def sb(name, shape, dt=F32):
            return ctx.enter_context(nc.sbuf_tensor(name, shape, dt))

        def sem(name):
            return ctx.enter_context(nc.semaphore(name))

        def bank(name):
            return ctx.enter_context(nc.psum_tensor(name, [P, 512], F32))

        MASK_C = TILES * PAIR
        const = sb("const", [P, P + MASK_C + P // HEAD])
        ident = const[:, 0:P]
        head_mask = const[:, P:P + MASK_C]
        head_ones = const[:, P + MASK_C:P + MASK_C + P // HEAD]
        w_raw = sb("w_raw", [P, KD, 4 * D])
        w_hi = sb("w_hi", [P, KD, 4 * D], F32R)
        w_lo = sb("w_lo", [P, KD, 4 * D], F32R)
        norm_rows = sb("norm_rows", [2 * KD, P])
        norm_cols = sb("norm_cols", [P, 2 * KD])
        n_scale, n_bias = norm_cols[:, 0:KD], norm_cols[:, KD:2 * KD]
        vec_rows = sb("vec_rows", [5 * KD, P])
        cols = sb("cols", [P, 5 * KD])
        f_scale, f_bias, emb_b, v_raw = (cols[:, i * KD:(i + n) * KD] for i, n in ((0, 1), (1, 1), (2, 2), (4, 1)))
        v_bias = sb("v_bias", [P, KD])
        nb_wide = sb("nb_wide", [P, KD, ROWS])
        b_raw = sb("b_raw", [ROWS, 2 * D])
        b_full = sb("b_full", [ROWS, 2 * D])
        wv_full = sb("wv_full", [P, KD, D])
        o_bias = sb("o_bias", [P, D])
        b_rows = sb("b_rows", [ROWS, 2 * D], F32R)
        one_rows = sb("one_rows", [ROWS, P], F32R)
        kt_rows = sb("kt_rows", [65, D], F32R)
        tok_rows = sb("tok_rows", [65, B * T], F32R)
        MASK_P = B * T // P
        mask_raw = sb("mask_raw", [MASK_P, P], I32)
        mask_row = sb("mask_row", [MASK_P, P], F32R)
        film_raw = sb("film_raw", [P, KE, 2 * D])
        cond_s = sb("cond_s", [B, E])
        cond_t = sb("cond_t", [B, E])
        cond_silu = sb("cond_silu", [B, E])
        condT = sb("condT", [P, KE, B])
        emb_rows = sb("emb_rows", [P, P])
        emb_bias = sb("emb_bias", [P, 2 * KD])
        emb_t = sb("emb_t", [P, 2 * KD, B])
        emb_half = sb("emb_half", [P, 2 * KD, B])
        emb = sb("emb", [P, 2 * KD, B])
        f_shift = sb("f_shift", [P, KD, B])
        film_g = sb("film_g", [P, KD, B])
        film_s = sb("film_s", [P, KD, B])
        power = sb("power", [P, TILES])
        tables = sb("tables", [P, TILES])

        x_all = sb("x_all", [P, UNITS * TILES * D])

        def x_tile(u, j):
            return x_all[:, bass.ds(u.times(TILES * D, j * D), D)]

        def x_of(u):
            return x_all[:, bass.ds(u.times(TILES * D), TILES * D)].rearrange("p (j d) -> p j d", d=D)

        def two(name, shape, dt=F32):
            return [sb(f"{name}{i}", shape, dt) for i in range(2)]

        bn = two("bn", [P, TILES, 6])
        mv = two("mv", [P, TILES, 2])
        var_e = two("var_e", [P, TILES])
        neg_rstd = two("neg_rstd", [P, TILES])
        rstd = two("rstd", [P, TILES])
        shift = two("shift", [P, TILES])
        z = two("z", [P, TILES, D])
        z_hi = two("z_hi", [P, KD, UT], F32R)
        z_lo = two("z_lo", [P, KD, UT], F32R)
        k_max = two("k_max", [P, KD * UB])
        k_sum = two("k_sum", [P, KD * UB])
        k_rec = two("k_rec", [P, KD * UB])
        k_exp = two("k_exp", [P, KD, UT])
        k_soft = two("k_soft", [P, KD, UT])
        q_max = two("q_max", [P, TILES, H])
        q_sub = two("q_sub", [P, TILES, D])
        q_exp = two("q_exp", [P, TILES, D])
        v = two("v", [P, TILES, D])
        qk_t = two("qk_t", [P, TILES, 2, KD, P])
        a_pair = two("a_pair", [P, TB, KD, TILES, PAIR])
        a_diag = two("a_diag", [P, TB, KD, TILES, P + G * 2])
        q_rec = two("q_rec", [P, TILES, H])
        y = two("y", [P, TILES, D])
        bn2 = two("bn2", [P, TILES, 6])
        mv2 = two("mv2", [P, TILES, 2])
        var_e2 = two("var_e2", [P, TILES])
        neg_rstd2 = two("neg_rstd2", [P, TILES])
        rstd2 = two("rstd2", [P, TILES])
        shift2 = two("shift2", [P, TILES])
        yn = two("yn", [P, TILES, D])
        h_scaled = two("h_scaled", [P, KD, UT])
        hp = two("hp", [P, KD, UT])
        th = two("th", [P, KD, UT])
        h2 = two("h2", [P, KD, UT])
        h_hi = two("h_hi", [P, KD, UT], F32R)
        h_lo = two("h_lo", [P, KD, UT], F32R)

        ps_z, ps_k = bank("ps_z"), bank("ps_k")
        ps_qv, ps_t, ps_yo = (ctx.enter_context(nc.psum_tensor(name, [P, 2, 512], F32))
                              for name in ("ps_qv", "ps_t", "ps_yo"))
        YC = P + G * 2

        s_norm, s_normps, s_vec, s_vecs, s_bk, s_wq, s_wv, s_embcopy, s_tables = map(
            sem, ["s_norm", "s_normps", "s_vec", "s_vecs", "s_bk", "s_wq", "s_wv", "s_embcopy", "s_tables"])
        s_const, s_cols, s_wk, s_brow, s_wo, s_mask, s_cond, s_film = map(
            sem, ["s_const", "s_cols", "s_wk", "s_brow", "s_wo", "s_mask", "s_cond", "s_film"])
        s_ones, s_diag0, s_tok, s_bq, s_heads = map(sem, ["s_ones", "s_diag0", "s_tok", "s_bq", "s_heads"])
        s_zeros, s_power, s_whi, s_split, s_nbw, s_brps, s_bfull, s_brdy, s_krows, s_maskrow = map(
            sem, ["s_zeros", "s_power", "s_whi", "s_split", "s_nbw", "s_brps", "s_bfull", "s_brdy",
                  "s_krows", "s_maskrow"])
        s_split_v = sem("s_split_v")
        s_maskf, s_bhi, s_ob, s_vbias, s_emb, s_embt = map(
            sem, ["s_maskf", "s_bhi", "s_ob", "s_vbias", "s_emb", "s_embt"])
        s_ctanh, s_csilu, s_ctps, s_ct, s_fps, s_f1, s_filmdone = map(
            sem, ["s_ctanh", "s_csilu", "s_ctps", "s_ct", "s_fps", "s_f1", "s_filmdone"])
        x_in = [sem("x_in0"), sem("x_in1")]
        r_biased = sem("r_biased")
        stored = sem("stored")
        bn_done, stats_x, var_x, rstd_x, neg_x, shift_x, z_done = map(
            sem, ["bn_done", "stats_x", "var_x", "rstd_x", "neg_x", "shift_x", "z_done"])
        zt_full, zhi_done, zlo_done = map(sem, ["zt_full", "zhi_done", "zlo_done"])
        kt_full, kmax_done, kexp_done, krec_done, ksoft_done = map(
            sem, ["kt_full", "kmax_done", "kexp_done", "krec_done", "ksoft_done"])
        qv_full, qmax_done, qsub_done, qexp_done, v_done = map(
            sem, ["qv_full", "qmax_done", "qsub_done", "qexp_done", "v_done"])
        t_full, t_read = map(sem, ["t_full", "t_read"])
        a_full, a_read, diag_act, diag_dve = map(sem, ["a_full", "a_read", "diag_act", "diag_dve"])
        y_full, qrec_done, y_read = map(sem, ["y_full", "qrec_done", "y_read"])
        bn2_done, stats_y, var_y, rstd_y, neg_y, shift_y, yn_done = map(
            sem, ["bn2_done", "stats_y", "var_y", "rstd_y", "neg_y", "shift_y", "yn_done"])
        h_full, film_mul, film_add, tanh_done, silu_done, hhi_done, hlo_done = map(
            sem, ["h_full", "film_mul", "film_add", "tanh_done", "silu_done", "hhi_done", "hlo_done"])
        o_full, res_done = map(sem, ["o_full", "res_done"])
        half_h, half_mul, half_add, half_tanh, half_silu, half_hi, half_lo_penult, half_lo_last = map(
            sem, ["half_h", "half_mul", "half_add", "half_tanh", "half_silu", "half_hi", "half_lo_penult",
                  "half_lo_last"])

        block = ctx.enter_context(nc.Block())

        def of(u, *stages):
            if u.within(UNITS):
                for stage in stages:
                    stage(u)

        def steps(engine, head, step, tail):
            head()
            for s in range(1, LOOP[0]):
                step(Unit(s // 2, s % 2))
            with engine.Fori(LOOP[0] // 2, LOOP[1] // 2) as pair:
                step(Unit(pair, 0))
                step(Unit(pair, 1))
            for s in range(LOOP[1], UNITS - 1):
                step(Unit(s // 2, s % 2))
            tail()

        first, second = Unit(0, 0), Unit(0, 1)
        fourth, third, penult, last_unit = [Unit((UNITS - n) // 2, (UNITS - n) % 2) for n in (4, 3, 2, 1)]

        h_t = ps_t[:, :, 0:UT]
        h_k = ps_k[:].rearrange("p (k t) -> p k t", k=KD)

        def half(u, k):
            return (KD if u is last_unit else 0) + k + 1

        def o_of(bank):
            return bank[:].rearrange("p (j c) -> p j c", j=TILES)

        def diagonal(u, g):
            r = slice(g * PAIR, (g + 1) * PAIR)
            return (a_diag[u.side][r, :, :, :, r].rearrange("p i k j c -> p (i k j) c"),
                    a_pair[u.side][r].rearrange("p i k j c -> p (i k j) c"))

        @block.sync
        def _(sp):
            def load_x(u):
                wait(sp, x_in[u.side], u.pair * 16)
                sp.dma_start(x_of(u), x_u[:, u.times(1)]).then_inc(x_in[u.side], 16)

            load_x(Unit(0, 0))
            for i, vec in ((0, norm_scale), (1, norm_bias)):
                sp.dma_start(norm_rows[i * KD:(i + 1) * KD, :],
                             vec.rearrange("(k p) -> k p", p=P)).then_inc(s_norm, 16)
            sp.dma_start(w_raw[:, :, K0:K0 + D], wk.rearrange("(k p) n -> p k n", p=P)).then_inc(s_wk, 16)
            sp.dma_start(b_raw[:, D:2 * D],
                         bk.rearrange("(a n) -> a n", a=1).to_broadcast([ROWS, D])).then_inc(s_bk, 16)
            sp.dma_start(mask_raw[:], mask.rearrange("(a b) t -> a (b t)", a=MASK_P)).then_inc(s_mask, 16)
            sp.dma_start(w_raw[:, :, 0:D], wq.rearrange("(k p) n -> p k n", p=P)).then_inc(s_wq, 16)
            sp.dma_start(b_raw[:, 0:D],
                         bq.rearrange("(a n) -> a n", a=1).to_broadcast([ROWS, D])).then_inc(s_brow, 16)
            sp.dma_start(w_raw[:, :, V0:V0 + D], wv.rearrange("(k p) n -> p k n", p=P)).then_inc(s_wv, 16)
            load_x(Unit(0, 1))
            sp.dma_start(cond_s[:], cond).then_inc(s_cond, 16)
            for i, vec, n in ((0, film_scale, KD), (1, film_bias, KD), (2, film_b, 2 * KD), (4, bv, KD)):
                sp.dma_start(vec_rows[i * KD:i * KD + n, :], vec.rearrange("(k p) -> k p", p=P)).then_inc(s_vec, 16)
            load_x(Unit(1, 0))
            sp.dma_start(film_raw[:], film_w.rearrange("(k p) n -> p k n", p=P)).then_inc(s_film, 16)
            sp.dma_start(w_raw[:, :, O0:O0 + D], out_w.rearrange("(k p) n -> p k n", p=P)).then_inc(s_wo, 16)
            sp.dma_start(o_bias[:], out_b.rearrange("(a n) -> a n", a=1).to_broadcast([P, D])).then_inc(s_ob, 16)
            for n in range(3, UNITS):
                load_x(Unit(n // 2, n % 2))

            def store(u):
                wait(sp, res_done, u.times(1, 1))
                sp.dma_start(out_u[:, u.times(1)], x_of(u)).then_inc(stored, 16)

            def step(s):
                of(s.back(3), store)

            def tail():
                for s in range(UNITS - 1, STEPS):
                    step(Unit(s // 2, s % 2))

            steps(sp, lambda: step(first), step, tail)
            sp.wait_ge(stored, 16 * UNITS)

        @block.gpsimd
        def _(pool):
            nc.gpsimd.memset(power[:], -0.5).then_inc(s_power, 1)
            nc.gpsimd.memset(kt_rows[:].bitcast(F32), 0.0).then_inc(s_zeros, 1)
            nc.gpsimd.memset(one_rows[:].bitcast(F32), 0.0).then_inc(s_zeros, 1)
            pool.wait_ge(s_zeros, 2)
            for row in (0, 32):
                nc.gpsimd.memset(one_rows[row:row + 1, :].bitcast(F32), 1.0).then_inc(s_ones, 1)
            nc.gpsimd.memset(kt_rows[64:65, :].bitcast(F32), 1.0).then_inc(s_ones, 1)

            def scale_and_shift(u, stats, mv_t, var, var_done, scale, scale_done, negative, negative_done,
                                offset, offset_done, used):
                wait(pool, stats, u.times(1, 1))
                wait(pool, used, u.times(1, -1))
                nc.gpsimd.tensor_scalar(var[u.side][:], mv_t[u.side][:, :, 1], EPS, None,
                                        ALU.add).then_inc(var_done, 1)
                wait(pool, var_done, u.times(1, 1))
                nc.gpsimd.tensor_tensor(scale[u.side][:], var[u.side][:], power[:], ALU.pow).then_inc(scale_done, 1)
                wait(pool, scale_done, u.times(1, 1))
                nc.gpsimd.tensor_scalar(negative[u.side][:], scale[u.side][:], -1.0, None,
                                        ALU.mult).then_inc(negative_done, 1)
                wait(pool, negative_done, u.times(1, 1))
                nc.gpsimd.tensor_tensor(offset[u.side][:], mv_t[u.side][:, :, 0], negative[u.side][:],
                                        ALU.mult).then_inc(offset_done, 1)

            def z_of(u):
                scale_and_shift(u, stats_x, mv, var_e, var_x, rstd, rstd_x, neg_rstd, neg_x, shift, shift_x, z_done)
                wait(pool, shift_x, u.times(1, 1))
                wait(pool, zt_full, u.times(1, -1))
                for j in range(TILES):
                    last = nc.gpsimd.tensor_scalar(z[u.side][:, j], x_tile(u, j), rstd[u.side][:, j:j + 1],
                                                   shift[u.side][:, j:j + 1], ALU.mult, ALU.add)
                last.then_inc(z_done, 1)

            pool.wait_ge(s_power, 1)
            pool.wait_ge(s_ones, 3)
            z_of(Unit(0, 0))
            for side in range(2):
                last = nc.gpsimd.memset(a_diag[side][:], 0.0)
            last.then_inc(s_diag0, 1)
            pool.wait_ge(s_whi, 3)
            nc.gpsimd.tensor_tensor(w_lo[:, :, V0:V0 + D], wv_full[:], w_hi[:, :, V0:V0 + D].bitcast(F32),
                                    ALU.subtract).then_inc(s_split_v, 1)
            z_of(Unit(0, 1))

            def y_scale(u):
                scale_and_shift(u, stats_y, mv2, var_e2, var_y, rstd2, rstd_y, neg_rstd2, neg_y, shift2, shift_y,
                                yn_done)

            def film_shift(u):
                wait(pool, film_mul, u.times(1, 1))
                wait(pool, silu_done, u.times(1, -1))
                nc.gpsimd.tensor_tensor(
                    hp[u.side][:].rearrange("p k (b t) -> p k b t", t=T),
                    h_scaled[u.side][:].rearrange("p k (b t) -> p k b t", t=T),
                    film_s[:, :, bass.ds(u.times(UB), UB), None].to_broadcast([P, KD, UB, T]),
                    ALU.add).then_inc(film_add, 1)

            def softmax_k(u):
                wait(pool, krec_done, u.times(1, 1))
                wait(pool, t_full, u.times(TILES, -TILES))
                nc.gpsimd.tensor_tensor(
                    k_soft[u.side][:].rearrange("p k (b t) -> p (k b) t", t=T),
                    k_exp[u.side][:].rearrange("p k (b t) -> p (k b) t", t=T),
                    k_rec[u.side][:, :, None].to_broadcast([P, KD * UB, T]), ALU.mult).then_inc(ksoft_done, 1)

            def silu_low(u):
                wait(pool, hhi_done, u.times(1, 1))
                wait(pool, o_full, u.times(1, -1))
                nc.gpsimd.tensor_tensor(h_lo[u.side][:], h2[u.side][:], h_hi[u.side][:].bitcast(F32),
                                        ALU.subtract).then_inc(hlo_done, 1)

            def bias_residual(u):
                if u.first():
                    pool.wait_ge(s_ob, 16)
                nc.gpsimd.tensor_tensor(x_of(u), x_of(u), o_bias[:, None, :].to_broadcast([P, TILES, D]),
                                        ALU.add).then_inc(r_biased, 1)

            def step(s):
                of(s.back(2), y_scale)
                of(s.back(-2), z_of)
                of(s.back(2), film_shift)
                of(s, softmax_k)
                of(s.back(2), bias_residual, silu_low)

            def film_setup():
                pool.wait_ge(s_vecs, 1)
                for part, shift in ((0, 1.0), (1, 0.0)):
                    at = slice(part * KD, (part + 1) * KD)
                    last = nc.gpsimd.tensor_scalar(emb_bias[:, at], emb_b[:, at], shift, None, ALU.add)
                last.then_inc(s_f1, 1)
                pool.wait_ge(s_embcopy, 1)
                nc.gpsimd.tensor_scalar(emb_half[:], emb_t[:], 0.5, None, ALU.mult).then_inc(s_f1, 1)
                pool.wait_ge(s_f1, 2)
                nc.gpsimd.tensor_tensor(emb[:], emb_half[:], emb_bias[:, :, None].to_broadcast([P, 2 * KD, B]),
                                        ALU.add).then_inc(s_f1, 1)
                pool.wait_ge(s_f1, 3)
                nc.gpsimd.tensor_tensor(f_shift[:], emb[:, 0:KD], f_bias[:, :, None].to_broadcast([P, KD, B]),
                                        ALU.mult).then_inc(s_f1, 1)
                nc.gpsimd.tensor_tensor(film_g[:], emb[:, 0:KD], f_scale[:, :, None].to_broadcast([P, KD, B]),
                                        ALU.mult).then_inc(s_filmdone, 1)
                pool.wait_ge(s_f1, 4)
                nc.gpsimd.tensor_tensor(film_s[:], f_shift[:], emb[:, KD:2 * KD], ALU.add).then_inc(s_filmdone, 1)

            def head():
                softmax_k(first)
                z_of(first.back(-2))
                film_setup()

            def tail():
                y_scale(third)
                softmax_k(last_unit)
                bias_residual(third)
                film_shift(third)
                bias_residual(penult)
                bias_residual(last_unit)
                y_scale(penult)
                silu_low(third)
                y_scale(last_unit)
                for k in range(KD):
                    pool.wait_ge(half_hi, half(penult, k))
                    nc.gpsimd.tensor_tensor(h_lo[penult.side][:, k], h2[penult.side][:, k],
                                            h_hi[penult.side][:, k].bitcast(F32),
                                            ALU.subtract).then_inc(half_lo_penult, 1)

            steps(pool, head, step, tail)

        @block.scalar
        def _(act):
            act.dma_start(const[:], consts).then_inc(s_const, 16)

            def weights_high(c):
                for k in range(KD):
                    last = nc.scalar.activation(w_hi[:, k, c:c + D], w_raw[:, k, c:c + D], ACT.Copy,
                                                scale=n_scale[:, k:k + 1])
                last.then_inc(s_whi, 1)

            def z_high(u):
                wait(act, zt_full, u.times(1, 1))
                wait(act, qv_full, u.times(TILES, -TILES))
                nc.scalar.activation(z_hi[u.side][:], ps_z[:].rearrange("p (k t) -> p k t", k=KD),
                                     ACT.Copy).then_inc(zhi_done, 1)

            act.wait_ge(s_power, 1)
            nc.scalar.activation(tables[:], power[:], ACT.Exp).then_inc(s_tables, 1)
            act.wait_ge(s_cols, 1)
            act.wait_ge(s_wk, 16)
            weights_high(K0)
            act.wait_ge(s_wq, 16)
            weights_high(0)
            act.wait_ge(s_maskf, 1)
            act.wait_ge(s_tok, 1)
            act.dma_start(tok_rows[64:65, :].bitcast(F32), mask_row[:].bitcast(F32)).then_inc(s_maskrow, 16)
            z_high(Unit(0, 0))
            act.wait_ge(s_wv, 16)
            for k in range(KD):
                nc.scalar.activation(wv_full[:, k], w_raw[:, k, V0:V0 + D], ACT.Copy, scale=n_scale[:, k:k + 1])
            weights_high(V0)
            act.wait_ge(s_cond, 16)
            nc.scalar.activation(cond_t[:], cond_s[:], ACT.Tanh, scale=0.5).then_inc(s_ctanh, 1)

            def v_of(u, j):
                wait(act, qsub_done, u.times(TILES, j + 1))
                wait(act, a_full, u.times(1, -1))
                nc.scalar.activation(v[u.side][:, j], ps_qv[:, j, V0:V0 + D], ACT.Copy).then_inc(v_done, 1)

            def transposed(u):
                wait(act, y_full, u.times(1, -1))
                for j in range(TILES):
                    wait(act, t_full, u.times(TILES, j + 1))
                    nc.scalar.activation(qk_t[u.side][:, j].rearrange("p a k t -> p (a k t)"), ps_t[:, j],
                                         ACT.Copy).then_inc(t_read, 1)

            def y_normalised(u):
                wait(act, shift_y, u.times(1, 1))
                wait(act, h_full, u.times(1, -1))
                for j in range(TILES):
                    last = nc.scalar.activation(yn[u.side][:, j], y[u.side][:, j], ACT.Identity,
                                                bias=shift2[u.side][:, j:j + 1], scale=rstd2[u.side][:, j:j + 1])
                last.then_inc(yn_done, 1)

            def k_exponential(u):
                wait(act, kmax_done, u.times(1, 1))
                wait(act, ksoft_done, u.times(1, -1))
                for k in range(KD):
                    for b in range(UB):
                        n = k * UB + b
                        last = nc.scalar.activation(
                            k_exp[u.side][:, k, b * T:(b + 1) * T], ps_k[:, n * T:(n + 1) * T], ACT.Exp,
                            bias=k_max[u.side][:, n:n + 1], accum_out=k_sum[u.side][:, n:n + 1])
                last.then_inc(kexp_done, 1)

            def diagonal_blocks(u):
                wait(act, a_read, u.times(1, 1))
                wait(act, y_full, u.times(1, -1))
                nc.scalar.activation(*diagonal(u, G - 1), ACT.Copy).then_inc(diag_act, 1)

            def silu_tanh(u):
                wait(act, film_add, u.times(1, 1))
                nc.scalar.activation(th[u.side][:], hp[u.side][:], ACT.Tanh, scale=0.5).then_inc(tanh_done, 1)

            def q_exponential(u):
                wait(act, qsub_done, u.times(TILES, TILES))
                wait(act, t_full, u.times(TILES, -TILES))
                nc.scalar.activation(q_exp[u.side][:], q_sub[u.side][:], ACT.Exp).then_inc(qexp_done, 1)

            def silu_high(u):
                wait(act, silu_done, u.times(1, 1))
                wait(act, o_full, u.times(1, -1))
                nc.scalar.activation(h_hi[u.side][:], h2[u.side][:], ACT.Copy).then_inc(hhi_done, 1)

            def step(s):
                of(s.back(1), transposed)
                of(s.back(-1), z_high)
                of(s.back(2), y_normalised)
                of(s, k_exponential)
                v_of(s, 0)
                of(s.back(1), diagonal_blocks)
                of(s.back(2), silu_tanh)
                q_exponential(s)
                v_of(s, 1)
                of(s.back(2), silu_high)

            def head():
                k_exponential(first)
                act.wait_ge(s_ctps, 1)
                nc.scalar.activation(condT[:], ps_yo[:, 1, 0:KE * B].rearrange("p (k b) -> p k b", k=KE),
                                     ACT.Copy).then_inc(s_ct, 1)
                nc.scalar.activation(cols[:], ps_yo[:, 1, P:P + 5 * KD], ACT.Copy).then_inc(s_vecs, 1)
                z_high(second)
                v_of(first, 0)
                q_exponential(first)
                v_of(first, 1)
                act.wait_ge(s_wo, 16)
                nc.scalar.activation(w_hi[:, :, O0:O0 + D], w_raw[:, :, O0:O0 + D], ACT.Copy,
                                     scale=0.5).then_inc(s_whi, 1)

            def tail():
                transposed(penult)
                k_exponential(last_unit)
                y_normalised(third)
                q_exponential(last_unit)
                diagonal_blocks(penult)
                v_of(last_unit, 0)
                v_of(last_unit, 1)
                transposed(last_unit)
                silu_tanh(third)
                diagonal_blocks(last_unit)
                silu_high(third)
                y_normalised(penult)
                for u in (penult, last_unit):
                    for k in range(KD):
                        act.wait_ge(half_add, half(u, k))
                        nc.scalar.activation(th[u.side][:, k], hp[u.side][:, k], ACT.Tanh,
                                             scale=0.5).then_inc(half_tanh, 1)
                    for k in range(KD):
                        act.wait_ge(half_silu, half(u, k))
                        nc.scalar.activation(h_hi[u.side][:, k], h2[u.side][:, k], ACT.Copy).then_inc(half_hi, 1)

            steps(act, head, step, tail)

        @block.vector
        def _(dve):
            def stats(u, src, ready, ready_at, bn_t, bn_sem):
                for j in range(TILES):
                    wait(dve, ready, ready_at[j])
                    nc.vector.bn_stats(bn_t[u.side][:, j], src(j)).then_inc(bn_sem, 1)

            def mean_variance(u, bn_t, bn_sem, mv_t, used, done):
                wait(dve, used, u.times(1, -1))
                for j in range(TILES):
                    wait(dve, bn_sem, u.times(TILES, j + 1))
                    last = nc.vector.bn_aggr(mv_t[u.side][:, j], bn_t[u.side][:, j])
                last.then_inc(done, 1)

            def x_stats(u):
                stats(u, lambda j: x_tile(u, j), x_in[u.side], [(u.pair + 1) * 16] * TILES, bn, bn_done)

            def x_mean(u):
                mean_variance(u, bn, bn_done, mv, shift_x, stats_x)

            def z_low(u):
                wait(dve, zhi_done, u.times(1, 1))
                nc.vector.tensor_tensor(z_lo[u.side][:], ps_z[:].rearrange("p (k t) -> p k t", k=KD),
                                        z_hi[u.side][:].bitcast(F32), ALU.subtract).then_inc(zlo_done, 1)

            def weights_low(c, at):
                dve.wait_ge(s_whi, at)
                for k in range(KD):
                    last = nc.vector.scalar_tensor_tensor(w_lo[:, k, c:c + D], w_raw[:, k, c:c + D],
                                                          n_scale[:, k:k + 1], w_hi[:, k, c:c + D].bitcast(F32),
                                                          ALU.mult, ALU.subtract)
                last.then_inc(s_split, 1)

            nc.vector.memset(tok_rows[:].bitcast(F32), 1.0).then_inc(s_tok, 1)
            x_stats(Unit(0, 0))
            x_mean(Unit(0, 0))
            dve.wait_ge(s_normps, 1)
            nc.vector.tensor_copy(norm_cols[:], ps_t[:, 0, 0:2 * KD]).then_inc(s_cols, 1)
            dve.wait_ge(s_cols, 1)
            for k in range(KD):
                last = nc.vector.tensor_copy(nb_wide[:, k], n_bias[:, k:k + 1].to_broadcast([P, ROWS]))
            last.then_inc(s_nbw, 1)
            dve.wait_ge(s_mask, 16)
            nc.vector.tensor_scalar(mask_row[:], mask_raw[:], 1.0, MASKED, ALU.is_equal,
                                    ALU.mult).then_inc(s_maskf, 1)
            weights_low(K0, 1)
            dve.wait_ge(s_bk, 16)
            dve.wait_ge(s_brps, 1)
            dve.wait_ge(s_ones, 3)
            kb = slice(D, 2 * D)
            nc.vector.tensor_tensor(b_full[:, kb], b_raw[:, kb], ps_yo[0:ROWS, 1, 0:D], ALU.add).then_inc(s_bfull, 1)
            dve.wait_ge(s_bfull, 1)
            nc.vector.tensor_copy(b_rows[:, kb], b_full[:, kb])
            nc.vector.tensor_copy(kt_rows[0:1, :], b_full[0:1, kb]).then_inc(s_bfull, 1)
            dve.wait_ge(s_bfull, 2)
            nc.vector.tensor_tensor(kt_rows[32:33, :], b_full[32:33, kb], b_rows[32:33, kb].bitcast(F32),
                                    ALU.subtract).then_inc(s_krows, 1)
            z_low(Unit(0, 0))

            def q_of(j):
                return ps_qv[:, j, 0:D].rearrange("p (h c) -> p h c", c=HEAD)

            def maximum(u, j):
                wait(dve, qv_full, u.times(TILES, j + 1))
                nc.vector.tensor_reduce(q_max[u.side][:, j], q_of(j), X, ALU.max).then_inc(qmax_done, 1)

            def less_maximum(u, j):
                wait(dve, qmax_done, u.times(TILES, j + 1))
                wait(dve, qexp_done, u.times(1, -1))
                nc.vector.tensor_tensor(q_sub[u.side][:, j].rearrange("p (h c) -> p h c", c=HEAD), q_of(j),
                                        q_max[u.side][:, j, :, None].to_broadcast([P, H, HEAD]),
                                        ALU.subtract).then_inc(qsub_done, 1)

            def k_maximum(u):
                wait(dve, kt_full, u.times(1, 1))
                wait(dve, kexp_done, u.times(1, -1))
                nc.vector.tensor_reduce(k_max[u.side][:], ps_k[:].rearrange("p (n t) -> p n t", t=T), X,
                                        ALU.max, negate=True).then_inc(kmax_done, 1)

            def residual(u, bank):
                wait(dve, o_full, u.times(1, 1))
                wait(dve, r_biased, u.times(1, 1))
                nc.vector.tensor_tensor(x_of(u), bank, x_of(u), ALU.add).then_inc(res_done, 1)

            def film_factor(u, bank=h_t):
                if u.first():
                    dve.wait_ge(s_filmdone, 1)
                wait(dve, h_full, u.times(1, 1))
                wait(dve, film_add, u.times(1, -1))
                nc.vector.tensor_tensor(
                    h_scaled[u.side][:].rearrange("p k (b t) -> p k b t", t=T),
                    bank.rearrange("p k (b t) -> p k b t", t=T),
                    film_g[:, :, bass.ds(u.times(UB), UB), None].to_broadcast([P, KD, UB, T]),
                    ALU.mult).then_inc(film_mul, 1)

            def k_reciprocal(u):
                wait(dve, kexp_done, u.times(1, 1))
                wait(dve, ksoft_done, u.times(1, -1))
                nc.vector.reciprocal(k_rec[u.side][:], k_sum[u.side][:]).then_inc(krec_done, 1)

            def a_masked(u, bank=ps_yo):
                wait(dve, a_full, u.times(1, 1))
                wait(dve, diag_act, u.times(1, -1))
                wait(dve, diag_dve, u.times(1, -1))
                if u.first():
                    dve.wait_ge(s_vbias, 1)
                for k in range(KD):
                    last = nc.vector.scalar_tensor_tensor(
                        a_pair[u.side][:, :, k].rearrange("p i j c -> p i (j c)"),
                        bank[:, :, k * MASK_C:(k + 1) * MASK_C], v_bias[:, k:k + 1],
                        head_mask[:, None, :].to_broadcast([P, TB, MASK_C]),
                        ALU.add, ALU.mult)
                last.then_inc(a_read, 1)

            def diagonal_blocks(u, groups):
                wait(dve, a_read, u.times(1, 1))
                wait(dve, y_full, u.times(1, -1))
                for g in groups:
                    last = nc.vector.tensor_copy(*diagonal(u, g))
                last.then_inc(diag_dve, 1)

            def silu(u):
                wait(dve, tanh_done, u.times(1, 1))
                wait(dve, hlo_done, u.times(1, -1))
                nc.vector.scalar_tensor_tensor(h2[u.side][:].rearrange("p k t -> p (k t)"),
                                               th[u.side][:].rearrange("p k t -> p (k t)"), 1.0,
                                               hp[u.side][:].rearrange("p k t -> p (k t)"),
                                               ALU.add, ALU.mult).then_inc(silu_done, 1)

            def q_reciprocal(u):
                wait(dve, y_full, u.times(1, 1))
                nc.vector.reciprocal(q_rec[u.side][:].rearrange("p j (k h) -> p j k h", k=KD),
                                     ps_yo[:, :, 0:KD * YC].rearrange("p j (k c) -> p j k c", c=YC)[:, :, :, P:YC]
                                     ).then_inc(qrec_done, 1)

            def y_of(u):
                wait(dve, qrec_done, u.times(1, 1))
                wait(dve, yn_done, u.times(1, -1))
                for j in range(TILES):
                    nc.vector.tensor_tensor(
                        y[u.side][:, j].rearrange("p (k h c) -> p k h c", k=KD, c=HEAD),
                        ps_yo[:, j, 0:KD * YC].rearrange("p (k c) -> p k c", c=YC)[:, :, 0:P]
                        .rearrange("p k (h c) -> p k h c", c=HEAD),
                        q_rec[u.side][:, j].rearrange("p (k h) -> p k h", k=KD)[:, :, :, None]
                        .to_broadcast([P, KD, H // KD, HEAD]), ALU.mult).then_inc(y_read, 1)

            def y_stats(u):
                stats(u, lambda j: y[u.side][:, j], y_read, [u.times(TILES, j + 1) for j in range(TILES)], bn2,
                      bn2_done)
                mean_variance(u, bn2, bn2_done, mv2, shift_y, stats_y)

            def y_normalised(u):
                wait(dve, rstd_y, u.times(1, 1))
                wait(dve, h_full, u.times(1, -1))
                for j in range(TILES):
                    last = nc.vector.tensor_scalar(yn[u.side][:, j], y[u.side][:, j], mv2[u.side][:, j, 0:1],
                                                   rstd2[u.side][:, j:j + 1], ALU.subtract, ALU.mult)
                last.then_inc(yn_done, 1)

            def film_half(u, k, dst, source, factors, op, ready, done):
                dve.wait_ge(ready, half(u, k))
                nc.vector.tensor_tensor(dst[u.side][:, k].rearrange("p (b t) -> p b t", t=T),
                                        source.rearrange("p (b t) -> p b t", t=T),
                                        factors[:, k, u.times(UB):u.times(UB, UB), None].to_broadcast([P, UB, T]),
                                        op).then_inc(done, 1)

            def film_halves(u):
                for k in range(KD):
                    film_half(u, k, h_scaled, ps_t[:, k, 0:UT], film_g, ALU.mult, half_h, half_mul)
                for k in range(KD):
                    film_half(u, k, hp, h_scaled[u.side][:, k], film_s, ALU.add, half_mul, half_add)

            def silu_halves(u):
                for k in range(KD):
                    dve.wait_ge(half_tanh, half(u, k))
                    nc.vector.scalar_tensor_tensor(h2[u.side][:, k], th[u.side][:, k], 1.0, hp[u.side][:, k],
                                                   ALU.add, ALU.mult).then_inc(half_silu, 1)

            def step(s):
                a, h = s.back(1), s.back(2)
                k_maximum(s)
                if a.first():
                    dve.wait_ge(s_embt, 1)
                    nc.vector.tensor_copy(emb_t[:], ps_yo[:, 1, 0:P].rearrange("p (c b) -> p c b", b=B)
                                          ).then_inc(s_embcopy, 1)
                of(s.back(-2), x_stats)
                of(s.back(-1), z_low)
                of(s.back(-2), x_mean)
                if s.back(3).within(UNITS):
                    residual(s.back(3), ps_yo[:, :, 0:D])
                maximum(s, 0)
                less_maximum(s, 0)
                of(h, film_factor)
                a_masked(a)
                k_reciprocal(s)
                diagonal_blocks(a, range(G - 1))
                maximum(s, 1)
                less_maximum(s, 1)
                if h.first():
                    dve.wait_ge(s_whi, 4)
                    nc.vector.scalar_tensor_tensor(w_lo[:, :, O0:O0 + D], w_raw[:, :, O0:O0 + D], 0.5,
                                                   w_hi[:, :, O0:O0 + D].bitcast(F32), ALU.mult,
                                                   ALU.subtract).then_inc(s_split, 1)
                of(h, silu)
                q_reciprocal(a)
                y_of(a)
                y_stats(a)

            def head():
                weights_low(0, 2)
                dve.wait_ge(s_brps, 2)
                dve.wait_ge(s_brow, 16)
                nc.vector.tensor_tensor(b_full[:, 0:D], b_raw[:, 0:D], ps_yo[0:ROWS, 0, 0:D],
                                        ALU.add).then_inc(s_bq, 1)
                dve.wait_ge(s_bq, 1)
                nc.vector.tensor_copy(b_rows[:, 0:D], b_full[:, 0:D]).then_inc(s_bhi, 1)
                x_stats(second)
                x_mean(second)
                k_maximum(first)
                dve.wait_ge(s_bhi, 1)
                nc.vector.tensor_tensor(b_rows[32:33, 0:D], b_full[32:33, 0:D], b_rows[32:33, 0:D].bitcast(F32),
                                        ALU.subtract).then_inc(s_brdy, 1)
                dve.wait_ge(s_ctanh, 1)
                nc.vector.scalar_tensor_tensor(cond_silu[:], cond_t[:], 1.0, cond_s[:], ALU.add,
                                               ALU.mult).then_inc(s_csilu, 1)
                maximum(first, 0)
                less_maximum(first, 0)
                x_stats(first.back(-2))
                k_reciprocal(first)
                x_mean(first.back(-2))
                maximum(first, 1)
                less_maximum(first, 1)
                z_low(second)
                dve.wait_ge(s_fps, 1)
                nc.vector.tensor_copy(emb_rows[:], ps_yo[:, 0, 0:P]).then_inc(s_emb, 1)
                dve.wait_ge(s_vecs, 1)
                nc.vector.tensor_tensor(v_bias[:], v_raw, ps_yo[:, 0, D:D + KD], ALU.add).then_inc(s_vbias, 1)
                dve.wait_ge(s_diag0, 1)
                for side in range(2):
                    last = nc.vector.tensor_copy(
                        a_diag[side][:, :, :, :, P:YC].rearrange("p i k j h -> p (i k j) h"),
                        head_ones[:, None, :].to_broadcast([P, TB * TILES * KD, P // HEAD]))
                last.then_inc(s_heads, 1)

            def tail():
                k_maximum(last_unit)
                maximum(last_unit, 0)
                less_maximum(last_unit, 0)
                maximum(last_unit, 1)
                k_reciprocal(last_unit)
                less_maximum(last_unit, 1)
                a_masked(penult)
                diagonal_blocks(penult, range(G - 1))
                film_factor(third, h_k)
                q_reciprocal(penult)
                y_of(penult)
                a_masked(last_unit, ps_qv)
                diagonal_blocks(last_unit, range(G - 1))
                y_stats(penult)
                silu(third)
                q_reciprocal(last_unit)
                y_of(last_unit)
                y_stats(last_unit)
                residual(fourth, o_of(ps_z))
                film_halves(penult)
                y_normalised(last_unit)
                silu_halves(penult)
                film_halves(last_unit)
                silu_halves(last_unit)
                residual(third, o_of(ps_k))
                for k in range(KD):
                    dve.wait_ge(half_hi, half(last_unit, k))
                    nc.vector.tensor_tensor(h_lo[last_unit.side][:, k], h2[last_unit.side][:, k],
                                            h_hi[last_unit.side][:, k].bitcast(F32),
                                            ALU.subtract).then_inc(half_lo_last, 1)
                residual(penult, ps_qv[:, :, 0:D])
                residual(last_unit, ps_yo[:, :, 0:D])

            steps(dve, head, step, tail)

        @block.tensor
        def _(pe):
            def z_transposed(u):
                wait(pe, z_done, u.times(1, 1))
                wait(pe, zlo_done, u.times(1, 0))
                for k in range(KD):
                    for j in range(TILES):
                        last = nc.tensor.transpose(ps_z[:, k * UT + j * P:k * UT + (j + 1) * P],
                                                   z[u.side][:, j, k * P:(k + 1) * P], ident)
                last.then_inc(zt_full, 1)

            def parts(hi, lo, other_hi, other_lo):
                return ((hi, other_hi), (hi, other_lo), (lo, other_hi))

            pe.wait_ge(s_const, 16)
            pe.wait_ge(s_norm, 16 * 2)
            nc.tensor.transpose(ps_t[:, 0, 0:2 * KD], norm_rows[:], ident[0:2 * KD, 0:2 * KD]).then_inc(s_normps, 1)
            pe.wait_ge(s_nbw, 1)
            pe.wait_ge(s_wk, 16)
            for k in range(KD):
                last = nc.tensor.matmul(ps_yo[0:ROWS, 1, 0:D], nb_wide[:, k], w_raw[:, k, K0:K0 + D],
                                        start=k == 0, stop=k == KD - 1)
            last.then_inc(s_brps, 1)
            z_transposed(Unit(0, 0))
            pe.wait_ge(s_wq, 16)
            for k in range(KD):
                last = nc.tensor.matmul(ps_yo[0:ROWS, 0, 0:D], nb_wide[:, k], w_raw[:, k, 0:D],
                                        start=k == 0, stop=k == KD - 1)
            last.then_inc(s_brps, 1)

            def cond_transposed():
                pe.wait_ge(s_bq, 1)
                pe.wait_ge(s_csilu, 1)
                for k in range(KE):
                    nc.tensor.transpose(ps_yo[:, 1, k * B:(k + 1) * B], cond_silu[:, k * P:(k + 1) * P],
                                               ident[0:B, 0:B])
                pe.wait_ge(s_vec, 16 * 4)
                nc.tensor.transpose(ps_yo[:, 1, P:P + 5 * KD], vec_rows[:], ident[0:5 * KD, 0:5 * KD]
                                    ).then_inc(s_ctps, 1)

            def qv(u, j):
                wait(pe, qsub_done, u.times(TILES, j + 1 - TILES))
                wait(pe, v_done, u.times(TILES, j + 1 - TILES))
                if u.first():
                    pe.wait_ge(s_split, 2)
                    pe.wait_ge(s_split_v, 1)
                t = slice(j * P, (j + 1) * P)
                for k in range(KD):
                    for n, (a, w) in enumerate(parts(z_hi, z_lo, w_hi, w_lo)):
                        end = k == KD - 1 and n == 2
                        if end:
                            if u.first():
                                pe.wait_ge(s_brdy, 1)
                            nc.tensor.matmul(ps_qv[:, j, 0:D], one_rows[:], b_rows[:, 0:D], start=False, stop=False)
                        last = nc.tensor.matmul(ps_qv[:, j], a[u.side][:, k, t], w[:, k, 0:2 * D],
                                                start=k == 0 and n == 0, stop=end)
                last.then_inc(qv_full, 1)

            def k_transposed(u):
                wait(pe, zhi_done, u.times(1, 1))
                wait(pe, zlo_done, u.times(1, 1))
                wait(pe, kexp_done, u.times(1, 0))
                if u.first():
                    pe.wait_ge(s_split, 1)
                for c in range(KD):
                    dst = ps_k[:, c * UT:(c + 1) * UT]
                    ch = slice(K0 + c * P, K0 + (c + 1) * P)
                    for k in range(KD):
                        for n, (a, w) in enumerate(parts(z_hi, z_lo, w_hi, w_lo)):
                            nc.tensor.matmul(dst, w[:, k, ch], a[u.side][:, k], start=k == 0 and n == 0,
                                             stop=False)
                    if u.first():
                        pe.wait_ge(s_krows, 1)
                        pe.wait_ge(s_maskrow, 16)
                        pe.wait_ge(s_ones, 3)
                    last = nc.tensor.matmul(dst, kt_rows[:, c * P:(c + 1) * P],
                                            tok_rows[:, bass.ds(u.times(UT), UT)], start=False, stop=True)
                last.then_inc(kt_full, 1)

            def q_k_transposed(u):
                wait(pe, qexp_done, u.times(1, 1))
                wait(pe, ksoft_done, u.times(1, 1))
                wait(pe, film_mul, u.times(1, -2 if u is last_unit else -1))
                for j in range(TILES):
                    wait(pe, t_read, u.times(TILES, j + 1 - TILES))
                    for k in range(KD):
                        nc.tensor.transpose(ps_t[:, j, k * P:(k + 1) * P],
                                            q_exp[u.side][:, j, k * P:(k + 1) * P], ident)
                    for k in range(KD):
                        last = nc.tensor.transpose(ps_t[:, j, D + k * P:D + (k + 1) * P],
                                                   k_soft[u.side][:, k, j * P:(j + 1) * P], ident)
                    last.then_inc(t_full, 1)
                if u.first():
                    pe.wait_ge(s_emb, 1)
                    nc.tensor.transpose(ps_yo[:, 1, 0:P], emb_rows[:], ident).then_inc(s_embt, 1)

            def projection(u, bank):
                wait(pe, hhi_done, u.times(1, 1))
                if u.first():
                    pe.wait_ge(s_split, 3)
                t = [slice(j * P, (j + 1) * P) for j in range(TILES)]
                for j in range(TILES):
                    dst = bank[:, j]
                    for n, (a, w) in enumerate(parts(h_hi, h_lo, w_hi, w_lo)):
                        if n == 2:
                            wait(pe, hlo_done, u.times(1, 1))
                        for k in range(KD):
                            last = nc.tensor.matmul(dst, a[u.side][:, k, t[j]], w[:, k, O0:O0 + D],
                                                    start=n == 0 and k == 0, stop=n == 2 and k == KD - 1)
                last.then_inc(o_full, 1)

            def y_transposed(u, bank, last_t=None):
                wait(pe, yn_done, u.times(1, 1))
                for k in range(KD):
                    if last_t:
                        wait(pe, t_read, last_t.times(TILES, k + 1))
                    for j in range(TILES):
                        last = nc.tensor.transpose(bank[:, k, j * P:(j + 1) * P],
                                                   yn[u.side][:, j, k * P:(k + 1) * P], ident)
                last.then_inc(h_full, 1)

            def y_halves(u):
                wait(pe, yn_done, u.times(1, 1))
                for k in range(KD):
                    if u is last_unit:
                        pe.wait_ge(half_mul, half(penult, k))
                    for j in range(TILES):
                        last = nc.tensor.transpose(ps_t[:, k, j * P:(j + 1) * P],
                                                   yn[u.side][:, j, k * P:(k + 1) * P], ident)
                    last.then_inc(half_h, 1)

            def projection_halves(u, bank, half_lo):
                for k in range(KD):
                    pe.wait_ge(half_hi, half(u, k))
                    for w in (w_hi, w_lo):
                        for j in range(TILES):
                            nc.tensor.matmul(bank[:, j, 0:D], h_hi[u.side][:, k, j * P:(j + 1) * P],
                                             w[:, k, O0:O0 + D], start=k == 0 and w is w_hi, stop=False)
                for k in range(KD):
                    pe.wait_ge(half_lo, k + 1)
                    for j in range(TILES):
                        last = nc.tensor.matmul(bank[:, j, 0:D], h_lo[u.side][:, k, j * P:(j + 1) * P],
                                                w_hi[:, k, O0:O0 + D], start=False, stop=k == KD - 1)
                last.then_inc(o_full, 1)

            def a_blocks(u, bank):
                wait(pe, t_read, u.times(TILES, TILES))
                wait(pe, v_done, u.times(TILES, TILES))
                if u.first():
                    pe.wait_ge(s_embcopy, 1)
                    pe.wait_ge(s_vbias, 1)
                    pe.wait_ge(s_heads, 1)
                for j in range(TILES):
                    for k in range(KD):
                        for i in range(TB):
                            for g in range(G):
                                r = slice(i * T, (i + 1) * T)
                                c = slice(k * P + g * PAIR, k * P + (g + 1) * PAIR)
                                at = (k * TILES + j) * PAIR
                                last = nc.tensor.matmul(
                                    bank[g * PAIR:(g + 1) * PAIR, i, at:at + PAIR], v[u.side][r, j, c],
                                    qk_t[u.side][r, j, 1].rearrange("p k t -> p (k t)")[:, c],
                                    start=True, stop=True)
                last.then_inc(a_full, 1)

            def y_products(u):
                wait(pe, diag_dve, u.times(1, 1))
                for j in range(TILES):
                    for k in range(KD):
                        for i in range(TB):
                            r = slice(i * T, (i + 1) * T)
                            last = nc.tensor.matmul(ps_yo[r, j, k * YC:(k + 1) * YC],
                                                    qk_t[u.side][:, j, 0, k, r], a_diag[u.side][:, i, k, j],
                                                    start=True, stop=True)
                last.then_inc(y_full, 1)

            def step(s):
                a, h, o = s.back(1), s.back(2), s.back(3)
                k_transposed(s)
                q_k_transposed(a)
                z_transposed(s.back(-1))
                if o.within(UNITS):
                    wait(pe, y_read, h.times(TILES, TILES))
                    projection(o, ps_yo[:, :, 0:D])
                qv(s, 0)
                if h.within(UNITS):
                    y_transposed(h, h_t, a)
                wait(pe, y_read, a.times(TILES, 0))
                wait(pe, res_done, o.times(1, 1))
                a_blocks(a, ps_yo)
                qv(s, 1)
                wait(pe, diag_act, a.times(1, 1))
                y_products(a)

            def head():
                k_transposed(first)
                qv(first, 0)
                cond_transposed()
                qv(first, 1)
                z_transposed(second)
                pe.wait_ge(s_bq, 1)
                pe.wait_ge(s_wv, 16)
                for c in range(KD):
                    for k in range(KD):
                        last = nc.tensor.matmul(ps_yo[:, 0, D + c:D + c + 1],
                                                w_raw[:, k, V0 + c * P:V0 + (c + 1) * P],
                                                n_bias[:, k:k + 1], start=k == 0, stop=k == KD - 1)
                last.then_inc(s_brps, 1)
                pe.wait_ge(s_ct, 1)
                pe.wait_ge(s_film, 16)
                for k in range(KE):
                    for c in range(2 * KD):
                        last = nc.tensor.matmul(ps_yo[c * B:(c + 1) * B, 0, 0:P], condT[:, k],
                                                film_raw[:, k, c * P:(c + 1) * P], start=k == 0, stop=k == KE - 1)
                last.then_inc(s_fps, 1)

            def tail():
                k_transposed(last_unit)
                q_k_transposed(penult)
                for j in range(TILES):
                    qv(last_unit, j)
                wait(pe, y_read, third.times(TILES, TILES))
                a_blocks(penult, ps_yo)
                wait(pe, kexp_done, last_unit.times(1, 1))
                y_transposed(third, h_k)
                q_k_transposed(last_unit)
                wait(pe, diag_act, penult.times(1, 1))
                y_products(penult)
                wait(pe, qsub_done, last_unit.times(TILES, TILES))
                a_blocks(last_unit, ps_qv)
                projection(fourth, o_of(ps_z))
                wait(pe, y_read, penult.times(TILES, TILES))
                wait(pe, diag_act, last_unit.times(1, 1))
                y_products(last_unit)
                wait(pe, t_read, last_unit.times(TILES, TILES))
                y_halves(penult)
                wait(pe, film_mul, third.times(1, 1))
                projection(third, o_of(ps_k))
                y_halves(last_unit)
                wait(pe, a_read, last_unit.times(1, 1))
                projection_halves(penult, ps_qv, half_lo_penult)
                wait(pe, y_read, last_unit.times(TILES, TILES))
                projection_halves(last_unit, ps_yo, half_lo_last)

            steps(pe, head, step, tail)


_INS = ["x", "cond_2048", "mask_BxS_ik0", "L0_cond_norm_scale", "L0_cond_norm_bias", "L0_cond_Wq", "L0_cond_bq",
        "L0_cond_Wk", "L0_cond_bk", "L0_cond_Wv", "L0_cond_bv", "L0_cond_film_emb_W", "L0_cond_film_emb_b",
        "L0_cond_film_norm_scale", "L0_cond_film_norm_bias", "L0_cond_film_out_W", "L0_cond_film_out_b"]


def kernel(**inputs):
    import numpy as np
    import concourse.bacc as bacc
    from concourse.bass_utils import run_bass_kernel_spmd

    nc = bacc.Bacc("TRN2", target_bir_lowering=False, num_devices=1)
    arrays, args = {}, []
    for name in _INS:
        a = np.ascontiguousarray(inputs[name])
        arrays[name] = a
        args.append(nc.dram_tensor(name, a.shape, mybir.dt.from_np(a.dtype), kind="ExternalInput").ap())
    p, head = np.arange(128), 16
    consts = np.concatenate([np.eye(128), p[:, None] % 32 // head == np.arange(64)[None] % 32 // head,
                             p[:, None] // head == np.arange(128 // head)[None]], axis=1).astype(np.float32)
    arrays["consts"] = consts
    args.append(nc.dram_tensor("consts", consts.shape, F32, kind="ExternalInput").ap())
    shape = inputs["x"].shape
    args.append(nc.dram_tensor("out", shape, F32, kind="ExternalOutput").ap())
    build(nc, *args)
    return run_bass_kernel_spmd(nc, [arrays], core_ids=[0]).results[0]["out"]
```
